# Optimizing a Trainium2 kernel written in Bass

```python
import numpy as np
import jax
import jax.numpy as jnp

def _softmax(x, axis=-1):
    return jax.nn.softmax(x, axis=axis)

def _gelu(x):
    return jax.nn.gelu(x, approximate=True)

def _silu(x):
    return jax.nn.silu(x)

def _sigmoid(x):
    return jax.nn.sigmoid(x)

def _layernorm(x, axis=-1, eps=1e-05):
    m = jnp.mean(x, axis=axis, keepdims=True)
    v = jnp.var(x, axis=axis, keepdims=True)
    return (x - m) / jnp.sqrt(v + eps)

def _scatter_add(tgt, idx, src, axis=0):
    return tgt.at[idx].add(src)

def _segment_sum(src, seg, n):
    return jax.ops.segment_sum(src, seg, n)
kernel_name = 'mk_xattn_ffn_d1_seqx_r4_ace7ac'

def setup_inputs(seed: int=0):
    np.random.seed(seed)
    _w = jnp.asarray

    def _rec_inputs():
        import jax
        import jax.numpy as jnp
        _rk = jax.random.key(seed)
        x = -0.0002928 + 1 * jax.random.normal(jax.random.fold_in(_rk, 1), (64, 128, 256), jnp.float32)
        _lenS = 128 - jax.random.randint(jax.random.fold_in(_rk, 7), (64,), 0, max(1, 128 // 4) + 1, jnp.int32)
        _lenS2 = 128 - jax.random.randint(jax.random.fold_in(_rk, 8), (64,), 0, max(1, 128 // 4) + 1, jnp.int32)
        _ctx_768P = jax.random.normal(jax.random.fold_in(_rk, 11), (64, 16, 192), jnp.float32)
        _ctx_768c = jax.random.dirichlet(jax.random.fold_in(_rk, 511), 0.3 * jnp.ones((16,), jnp.float32), (64, 128))
        _ctx_768t = jnp.einsum('bsk,bkd->bsd', _ctx_768c, _ctx_768P)
        _ctx_768t = _ctx_768t * jax.lax.rsqrt(jnp.mean(jnp.square(_ctx_768t)) + 1e-12) * 0.953939
        ctx_768 = 2.09791e-05 + 1.00001 * (_ctx_768t + 0.3 * jax.random.normal(jax.random.fold_in(_rk, 611), (64, 128, 192), jnp.float32))
        return (x, ctx_768)
    x, ctx_768 = _rec_inputs()

    def _L0_xattn_setup():
        import jax, jax.numpy as jnp
        import numpy as np
        B, LQ, LKV = (2, 512, 512)
        C, CTX, H, DK = (256, 192, 16, 64)
        SCALE = DK ** (-0.5)
        key = jax.random.key(seed)
        kx, ky, kq, kkv, kp, kb = jax.random.split(key, 6)
        return {'x': jax.random.normal(kx, (B, LQ, C), dtype=jnp.float32), 'y': jax.random.normal(ky, (B, LKV, CTX), dtype=jnp.float32), 'Wq': jax.random.normal(kq, (C, H * DK), dtype=jnp.float32) * C ** (-0.5), 'Wkv': jax.random.normal(kkv, (CTX, 2 * H * DK), dtype=jnp.float32) * CTX ** (-0.5), 'Wproj': jax.random.normal(kp, (H * DK, C), dtype=jnp.float32) * (H * DK) ** (-0.5), 'bproj': jax.random.normal(kb, (C,), dtype=jnp.float32) * 0.01}
    _L0_xattn_all = _L0_xattn_setup()
    _L0_xattn_in = {k: v for k, v in _L0_xattn_all.items() if k in ('Wq', 'Wkv', 'Wproj', 'bproj')}
    del _L0_xattn_all

    def _L0_ffn_setup():
        import jax, jax.numpy as jnp
        import numpy as np
        HIDDEN = 256
        NUM_EXPERTS = 8
        BATCH, SEQ = (4, 1024)
        key = jax.random.key(seed)
        ks = jax.random.split(key, 6)
        s = 1.0 / np.sqrt(HIDDEN)
        tokens = jax.random.normal(ks[0], (BATCH, SEQ, HIDDEN), dtype=jnp.float32)
        gate_w = jax.random.uniform(ks[1], (NUM_EXPERTS, HIDDEN), jnp.float32, -s, s)
        expert_w = jax.random.uniform(ks[2], (NUM_EXPERTS, HIDDEN, HIDDEN), jnp.float32, -s, s)
        expert_b = jax.random.uniform(ks[3], (NUM_EXPERTS, HIDDEN), jnp.float32, -s, s)
        combine_w = jax.random.uniform(ks[4], (HIDDEN, HIDDEN), jnp.float32, -s, s)
        return {'tokens': tokens, 'gate_w': gate_w, 'expert_w': expert_w, 'expert_b': expert_b, 'combine_w': combine_w}
    _L0_ffn_all = _L0_ffn_setup()
    _L0_ffn_in = {k: v for k, v in _L0_ffn_all.items() if k in ('gate_w', 'expert_w', 'expert_b', 'combine_w')}
    del _L0_ffn_all
    return {'x': x, 'ctx_768': ctx_768, 'L0_xattn_Wq': _L0_xattn_in['Wq'], 'L0_xattn_Wkv': _L0_xattn_in['Wkv'], 'L0_xattn_Wproj': _L0_xattn_in['Wproj'], 'L0_xattn_bproj': _L0_xattn_in['bproj'], 'L0_ffn_gate_w': _L0_ffn_in['gate_w'], 'L0_ffn_expert_w': _L0_ffn_in['expert_w'], 'L0_ffn_expert_b': _L0_ffn_in['expert_b'], 'L0_ffn_combine_w': _L0_ffn_in['combine_w']}

def reference(x, ctx_768, L0_xattn_Wq, L0_xattn_Wkv, L0_xattn_Wproj, L0_xattn_bproj, L0_ffn_gate_w, L0_ffn_expert_w, L0_ffn_expert_b, L0_ffn_combine_w):
    import jax
    import jax.numpy as jnp

    def _L0_xattn_ref(x, y, Wq, Wkv, Wproj, bproj):
        import jax, jax.numpy as jnp
        import numpy as np
        B, LQ, LKV = (2, 512, 512)
        C, CTX, H, DK = (256, 192, 16, 64)
        SCALE = DK ** (-0.5)
        b, lq, _ = x.shape
        lkv = y.shape[1]
        q = (x @ Wq).reshape(b, lq, H, DK).transpose(0, 2, 1, 3)
        kv = (y @ Wkv).reshape(b, lkv, 2, H, DK).transpose(2, 0, 3, 1, 4)
        k, v = (kv[0], kv[1])
        atten = jax.nn.softmax(jnp.einsum('bhid,bhjd->bhij', q, k) * SCALE, axis=-1)
        res = jnp.einsum('bhij,bhjd->bhid', atten, v)
        res = res.transpose(0, 2, 1, 3).reshape(b, lq, H * DK)
        out = res @ Wproj + bproj
        return out

    def _L0_ffn_ref(tokens, gate_w, expert_w, expert_b, combine_w):
        import jax, jax.numpy as jnp
        import numpy as np
        HIDDEN = 256
        NUM_EXPERTS = 8
        BATCH, SEQ = (4, 1024)
        B, S, H = tokens.shape
        logits = jnp.einsum('bsh,eh->bse', tokens, gate_w)
        probs = jax.nn.softmax(logits, axis=-1)
        top2_w, top2_idx = jax.lax.top_k(probs, 2)
        flat = tokens.reshape(B * S, H)
        flat_idx = top2_idx.reshape(B * S, 2)
        flat_w = top2_w.reshape(B * S, 2)
        expert_out = jax.nn.silu(jnp.einsum('nh,edh->ned', flat, expert_w) + expert_b[None, :, :])
        gathered = jnp.take_along_axis(expert_out, flat_idx[:, :, None], axis=1)
        mixed = jnp.sum(gathered * flat_w[:, :, None], axis=1)
        out = jnp.einsum('bsh,dh->bsd', mixed.reshape(B, S, H), combine_w)
        return out
    x = x + _L0_xattn_ref(_layernorm(x, axis=-1), ctx_768, L0_xattn_Wq, L0_xattn_Wkv, L0_xattn_Wproj, L0_xattn_bproj)
    x = x + _L0_ffn_ref(_layernorm(x, axis=-1), L0_ffn_gate_w, L0_ffn_expert_w, L0_ffn_expert_b, L0_ffn_combine_w)
    return x

_drawn_inputs = setup_inputs


def setup_inputs(seed=0):
    import zlib

    import numpy as np

    out = dict(_drawn_inputs(seed))
    spreads = {}
    factors = {'L0_xattn_bproj': 5.794, 'L0_ffn_expert_b': 8.0}
    for name, (base, spread) in spreads.items():
        noise = np.random.default_rng([zlib.crc32(name.encode()), seed]).standard_normal(out[name].shape)
        drawn = base * np.exp(spread * noise) if base else spread * noise
        out[name] = jnp.asarray(drawn.astype(out[name].dtype))
    for name, factor in factors.items():
        out[name] = (out[name] * factor).astype(out[name].dtype)
    return out
```

```python
from contextlib import ExitStack

import concourse.bass as bass
from concourse import mybir

P = 128
F32 = mybir.dt.float32
F32R = mybir.dt.float32r
U32 = mybir.dt.uint32
ALU = mybir.AluOpType
ACT = mybir.ActivationFunctionType
AX_X = mybir.AxisListType.X

HALF = 64
HEAD_PAIRS = 8
SLOTS = HEAD_PAIRS
EPS = 1e-5

JOBS = [
    (0, "mid", "combine", 0, -3),
    (0, "late", "expert", 3, -2),
    (1, "mid", "value", 2, 0),
    (1, "late", "expert", 4, -2),
    (2, "mid", "value", 3, 0),
    (2, "late", "expert", 5, -2),
    (3, "mid", "turn_x1", 0, -1),
    (3, "late", "expert", 6, -2),
    (4, "mid", "gate", 0, -1),
    (4, "mid", "turn_x", 0, 1),
    (4, "late", "expert", 7, -2),
    (5, "mid", "turn_gate", 0, -1),
    (5, "mid", "value", 0, 1),
    (5, "late", "expert", 0, -1),
    (6, "mid", "value", 1, 1),
    (6, "late", "expert", 1, -1),
    (7, "mid", "turn_mixed", 0, -2),
    (7, "late", "expert", 2, -1),
]
BANKS = 3
PER_PAIR = {"expert": 8, "value": 4, "turn_x": 1, "turn_x1": 1, "gate": 1, "turn_gate": 1,
            "turn_mixed": 1, "combine": 1}


def plus(j, n):
    return j + n if n else j


def nth(j, per, k):
    return plus(j * per if per != 1 else j, k + 1)


def exists(j, pairs):
    return not isinstance(j, int) or 0 <= j < pairs


def wait(eng, sem, count):
    if not isinstance(count, int) or count > 0:
        eng.wait_ge(sem, count)


def steps(eng, pairs, step):
    for i in (-1, 0, 1, 2, 3):
        step(i, i % 2)
    with eng.Fori(4, pairs - 3, 2) as i:
        step(i, 0)
        step(i + 1, 1)
    for i in (pairs - 2, pairs - 1, pairs, pairs + 1, pairs + 2):
        step(i, i % 2)


def xattn_moe_kernel(nc, x, ctxT, wq, wkv, wkv_rest, wproj, bproj, gateT, expertT, expert_b, combineT, out):
    pairs = x.shape[0] // (2 * P)
    C = x.shape[1]
    D = wq.shape[1]
    E = gateT.shape[1]
    N2 = 2 * P

    x_pairs = x.rearrange("(j t p) c -> j p t c", t=2, p=P)
    out_pairs = out.rearrange("(j t p) c -> j p t c", t=2, p=P)

    with ExitStack() as stack:
        def sb(name, shape, dt=F32):
            return stack.enter_context(nc.sbuf_tensor(name, shape, dt))

        def sem(name):
            return stack.enter_context(nc.semaphore(name))

        def hilo(name, shape):
            return [sb(name + "_hi", shape, F32R), sb(name + "_lo", shape, F32R)]

        wq_s = hilo("wq_s", [P, 2, D])
        wkv0_s = hilo("wkv0_s", [P, 2 * D])
        wkvr_s = hilo("wkvr_s", [P, 2 * D])
        wproj_s = hilo("wproj_s", [P, HEAD_PAIRS, C])
        wexp_s = hilo("wexp_s", [P, 2, E * C])
        wcomb_s = hilo("wcomb_s", [P, 2, C])
        wgate = sb("wgate", [P, 2, P], F32R)
        gate_raw = sb("gate_raw", [P, 2, E])
        ebias = sb("ebias", [P, E * C])
        pbias = sb("pbias", [P, C])
        ident = sb("ident", [P, P])
        minus_half = sb("minus_half", [P, 2])
        eps = sb("eps", [P, 2])
        expert_no = sb("expert_no", [P, E])

        x_raw = sb("x_raw", [P, 2, C])
        c_raw = sb("c_raw", [P, 2, N2])
        xT = [hilo(f"xT{b}", [P, 2, N2]) for b in range(2)]
        cT = [(sb(f"cT{b}_hi", [P, 2, N2], F32R), sb(f"cT{b}_lo", [P, N2], F32R)) for b in range(2)]
        v_s = hilo("v_s", [P, 2, D])
        q_s = [hilo(f"q_s{b}", [P, N2]) for b in range(2)]
        k_s = [hilo(f"k_s{b}", [P, 2, N2]) for b in range(2)]
        probs = [sb(f"probs{b}", [P, 4, P]) for b in range(2)]
        pT_s = hilo("pT_s", [P, 4 * P])
        o_s = [hilo(f"o_s{b}", [P, 2, P]) for b in range(2)]
        xb = sb("xb", [P, 2, C])
        x1 = [sb(f"x1_{b}", [P, 2, C]) for b in range(2)]
        x1T = [hilo(f"x1T{b}", [P, 2, N2]) for b in range(2)]
        mT_s = hilo("mT_s", [P, 2, N2])
        outb = sb("outb", [P, 2, C])
        gate_s = sb("gate_s", [P, N2])
        scratch = sb("scratch", [P, 2, 2048])
        z = [scratch[:, 0, 0:512], scratch[:, 0, 512:1024]]
        th = [scratch[:, 0, 1024:1536], scratch[:, 0, 1536:2048]]
        acc = scratch[:, 1, 0:512]
        weighted = scratch[:, 1, 512:1024]
        mixed = scratch[:, 1, 1024:1536].rearrange("p (t c) -> p t c", t=2)
        xn2 = scratch[:, 1, 1536:2048].rearrange("p (t c) -> p t c", t=2)

        stats = [sb(f"stats{n}", [P, 2, 6]) for n in (1, 2)]
        mv = [sb(f"mv{n}", [P, 2, 2]) for n in (1, 2)]
        var_eps = [sb(f"var_eps{n}", [P, 2]) for n in (1, 2)]
        rstd = [sb(f"rstd{n}", [P, 2]) for n in (1, 2)]
        neg_max = [sb(f"neg_max{b}", [P, 4]) for b in range(2)]
        sums = [sb(f"sums{b}", [P, 4]) for b in range(2)]
        inv_sums = [sb(f"inv_sums{b}", [P, 4]) for b in range(2)]
        logits = sb("logits", [P, 2, E])
        top8 = sb("top8", [P, 2, 8])
        top_at = sb("top_at", [P, 2, 8], U32)
        top_atf = sb("top_atf", [P, 2, 2])
        neg_top = sb("neg_top", [P, 2])
        gate_exp = sb("gate_exp", [P, 2, 8])
        gate_sum = sb("gate_sum", [P, 2])
        gate_inv = sb("gate_inv", [P, 2])
        top_w = sb("top_w", [P, 2, 2])
        chosen = sb("chosen", [P, 4, E])
        route_w = [sb(f"route_w{b}", [P, 2, E]) for b in range(2)]

        qk_ps = stack.enter_context(nc.psum_tensor("qk_ps", [P, 512], F32))
        s_ps = stack.enter_context(nc.psum_tensor("s_ps", [P, 512], F32))
        pT_ps = stack.enter_context(nc.psum_tensor("pT_ps", [P, 512], F32))
        o_ps = stack.enter_context(nc.psum_tensor("o_ps", [P, 512], F32))
        proj_ps = stack.enter_context(nc.psum_tensor("proj_ps", [P, 512], F32))
        gen_ps = [stack.enter_context(nc.psum_tensor(f"gen_ps{b}", [P, 512], F32)) for b in range(BANKS)]

        x_in, c_in, xres_in, small_in, out_stored = (
            sem(n) for n in ("x_in", "c_in", "xres_in", "small_in", "out_stored"))
        w_in = [sem(f"w_in{b}") for b in range(2)]
        const_a, const_b, zeroed = sem("const_a"), sem("const_b"), sem("zeroed")
        w_hi, w_lo_dve, w_lo_pool, gate_w_ready = (
            sem(n) for n in ("w_hi", "w_lo_dve", "w_lo_pool", "gate_w_ready"))
        qk_made, s_made, pT_made, o_made, proj_made = (
            sem(n) for n in ("qk_made", "s_made", "pT_made", "o_made", "proj_made"))
        made = {k: sem("made_" + k) for k in PER_PAIR}
        qk_hi, exp_done, pT_hi, o_hi, ctx_hi, tanh_done, tanh_plus, gate_exp_done = (
            sem(n) for n in ("qk_hi", "exp_done", "pT_hi", "o_hi", "ctx_hi", "tanh_done", "tanh_plus", "gate_exp_done"))
        hi_of = {k: sem("hi_" + k) for k in ("value", "turn_x", "turn_x1", "turn_mixed")}
        qk_lo, max_done, inv_done, pT_lo, o_lo, x1_done, xn_done, xn2_done, silu_done = (
            sem(n) for n in ("qk_lo", "max_done", "inv_done", "pT_lo", "o_lo", "x1_done", "xn_done",
                             "xn2_done", "silu_done"))
        drained = {k: sem("drained_" + k) for k in PER_PAIR}
        bn_done = [sem(f"bn_done{n}") for n in (1, 2)]
        mv_done = [sem(f"mv_done{n}") for n in (1, 2)]
        top_done, route_step, route_done = sem("top_done"), sem("route_step"), sem("route_done")
        ctx_rest = sem("ctx_rest")
        ctx_lo, probs_done, xb_done, mix_step, mix_done, mixed_done = (
            sem(n) for n in ("ctx_lo", "probs_done", "xb_done", "mix_step", "mix_done", "mixed_done"))
        eps_done = [sem(f"eps_done{n}") for n in (1, 2)]
        rstd_done = [sem(f"rstd_done{n}") for n in (1, 2)]

        block = stack.enter_context(nc.Block())

        def jobs(u, position, i):
            for n, (slot, pos, kind, k, off) in enumerate(JOBS):
                if slot == u and pos == position and exists(plus(i, off), pairs):
                    yield kind, k, plus(i, off), off, n % BANKS

        def bank_free(pe, i, n):
            m = n
            while True:
                m -= BANKS
                step_back = -(m // len(JOBS))
                _, _, kind, k, off = JOBS[m % len(JOBS)]
                j = plus(i, off - step_back)
                if exists(j, pairs):
                    pe.wait_ge(drained[kind], nth(j, PER_PAIR[kind], k))
                    return
                if isinstance(i, int) and i - step_back < -1:
                    return

        raw = [scratch[:, n % 2, :] for n in range(7)]
        WEIGHT_PIECES = [
            (wq.rearrange("(a p) n -> p a n", p=P), raw[0].rearrange("p (a n) -> p a n", a=2)),
            (wkv[0:P, :], raw[1]),
            (wkv_rest, raw[2]),
            (wproj.rearrange("(g p) n -> p g n", p=P), raw[3].rearrange("p (g n) -> p g n", g=HEAD_PAIRS)),
            (expertT[0:P, :], raw[4]),
            (expertT[P:2 * P, :], raw[5]),
            (combineT.rearrange("(a p) n -> p a n", p=P), raw[6][:, 0:2 * C].rearrange("p (a n) -> p a n", a=2)),
        ]
        flat = lambda ap, s: ap.rearrange(s)
        SPLIT = [
            [flat(w[:, :, :], "p a n -> p (a n)") for w in wq_s],
            [w[:, :] for w in wkv0_s],
            [w[:, :] for w in wkvr_s],
            [flat(w[:, :, :], "p g n -> p (g n)") for w in wproj_s],
            [w[:, 0, :] for w in wexp_s],
            [w[:, 1, :] for w in wexp_s],
            [flat(w[:, :, :], "p a n -> p (a n)") for w in wcomb_s],
        ]
        BY_VECTOR = 3
        QSCALE = float(HALF) ** -0.5

        def weight_hi(act, n):
            act.wait_ge(w_in[n % 2], 16 * (n // 2 + 1))
            hi = SPLIT[n][0]
            act.activation(hi, raw[n][:, 0:hi.shape[1]], ACT.Copy, scale=QSCALE if n == 0 else 1.0).then_inc(w_hi, 1)

        def weight_lo(eng, n, done):
            eng.wait_ge(w_hi, n + 1)
            hi, lo = SPLIT[n]
            if n == 0:
                eng.scalar_tensor_tensor(out=lo, in0=raw[n], scalar=QSCALE, in1=hi.bitcast(F32),
                                         op0=ALU.mult, op1=ALU.subtract).then_inc(done, 1)
            else:
                rows = HALF if n == 2 else P
                eng.tensor_tensor(lo[0:rows, :], raw[n][0:rows, 0:hi.shape[1]], hi[0:rows, :].bitcast(F32),
                                  ALU.subtract).then_inc(done, 1)

        @block.sync
        def _(sp):
            def load_x(j):
                wait(sp, made["turn_x"], j)
                sp.dma_start(x_raw[:, :, :], x_pairs[j]).then_inc(x_in, 16)

            def load_ctx(j):
                wait(sp, ctx_hi, j)
                wait(sp, ctx_lo, j)
                wait(sp, ctx_rest, j)
                sp.dma_start(c_raw[:, :, :], ctxT[j].rearrange("p (a n) -> p a n", a=2)).then_inc(c_in, 16)

            def load_weights(n):
                if n >= 2:
                    wait(sp, w_hi, n - 1)
                    wait(sp, w_lo_dve, min(n - 1, BY_VECTOR))
                    wait(sp, w_lo_pool, n - 1 - BY_VECTOR)
                to, of = WEIGHT_PIECES[n][1], WEIGHT_PIECES[n][0]
                sp.dma_start(to, of).then_inc(w_in[n % 2], 16)

            load_ctx(0)
            load_x(0)
            load_weights(1)
            load_weights(0)
            sp.dma_start(gate_raw[:, :, :], gateT.rearrange("(a p) e -> p a e", p=P)).then_inc(small_in, 16)
            sp.dma_start(pbias[:, :], bproj.partition_broadcast(P)).then_inc(small_in, 16)
            sp.dma_start(ebias[:, :], expert_b.partition_broadcast(P)).then_inc(small_in, 16)
            for n in range(2, 5):
                load_weights(n)

            def step(i, par):
                if isinstance(i, int) and i == 0:
                    load_weights(5)
                    load_weights(6)
                if exists(plus(i, -3), pairs):
                    sp.wait_ge(drained["combine"], i - 2)
                    sp.dma_start(out_pairs[i - 3], outb[:, :, :]).then_inc(out_stored, 16)
                if exists(i, pairs):
                    wait(sp, x1_done, i)
                    sp.dma_start(xb[:, :, :], x_pairs[i]).then_inc(xres_in, 16)
                if exists(i + 2, pairs):
                    load_ctx(i + 2)
                    load_x(i + 2)

            steps(sp, pairs, step)
            sp.wait_ge(out_stored, 16 * pairs)

        @block.tensor
        def _(pe):
            def products(out_ap, terms, start=True, stop=True, skip=False):
                for n, (l, r) in enumerate(terms):
                    mm = pe.matmul(out_ap, l, r, start=start and n == 0, stop=stop and n == len(terms) - 1,
                                   skip_group_check=skip)
                return mm

            def three(lhs, rhs, pick_l, pick_r):
                return [(pick_l(lhs[a]), pick_r(rhs[b])) for a, b in ((0, 0), (0, 1), (1, 0))]

            def queries_keys(j, p, par):
                if p == 0:
                    pe.wait_ge(drained["turn_x"], nth(j, 1, 0))
                if isinstance(j, int) and j == 0 and p == 0:
                    pe.wait_ge(w_hi, BY_VECTOR)
                    pe.wait_ge(w_lo_dve, BY_VECTOR)
                wait(pe, qk_lo, nth(j, HEAD_PAIRS, p - 1))
                cols = slice(p * P, (p + 1) * P)
                bank = qk_ps
                terms = []
                for a in range(2):
                    terms += three(wq_s, xT[par], lambda w: w[:, a, cols], lambda y: y[:, a, :])
                products(bank[:, 0:N2], terms)
                hi, lo = cT[par]
                products(bank[:, N2:2 * N2], [
                    (wkv0_s[0][:, cols], hi[:, 0, :]), (wkv0_s[0][:, cols], lo[:, :]), (wkv0_s[1][:, cols], hi[:, 0, :]),
                    (wkvr_s[0][:, cols], hi[:, 1, :]), (wkvr_s[1][:, cols], hi[:, 1, :]),
                ]).then_inc(qk_made, 1)

            def scores(j, p):
                pe.wait_ge(qk_lo, nth(j, HEAD_PAIRS, p))
                wait(pe, exp_done, nth(j, HEAD_PAIRS, p - 1))
                for t in range(2):
                    mm = products(s_ps[:, t * N2:(t + 1) * N2], three(
                        q_s[p % 2], k_s[p % 2], lambda q: q[:, t * P:(t + 1) * P], lambda k: k[:, t, :]))
                mm.then_inc(s_made, 1)

            def turn_probs(j, p):
                pe.wait_ge(probs_done, nth(j, HEAD_PAIRS, p))
                wait(pe, pT_lo, nth(j, HEAD_PAIRS, p - 1))
                for k in range(4):
                    mm = pe.transpose(pT_ps[:, k * P:(k + 1) * P], probs[p % 2][:, k, :], ident[:, :])
                mm.then_inc(pT_made, 1)

            def attend(j, p):
                pe.wait_ge(pT_lo, nth(j, HEAD_PAIRS, p))
                if p % 4 == 0:
                    pe.wait_ge(drained["value"], nth(j, 4, 2 * (p // 4) + 1))
                wait(pe, o_lo, nth(j, HEAD_PAIRS, p - 1))
                for t in range(2):
                    mm = products(o_ps[:, t * N2:(t + 1) * N2], three(
                        v_s, pT_s, lambda v: v[:, t, p * P:(p + 1) * P], lambda q: q[:, t * N2:(t + 1) * N2]))
                mm.then_inc(o_made, 1)

            def project(j, p):
                pe.wait_ge(o_lo, nth(j, HEAD_PAIRS, p))
                if p == 0:
                    wait(pe, x1_done, j)
                    if isinstance(j, int) and j == 0:
                        pe.wait_ge(w_lo_pool, 1)
                for t in range(2):
                    mm = products(proj_ps[:, t * C:(t + 1) * C], three(
                        o_s[p % 2], wproj_s, lambda o: o[:, t, :], lambda w: w[:, p, :]),
                        start=p == 0 and t == 0, stop=p == HEAD_PAIRS - 1, skip=True)
                mm.then_inc(proj_made, 1)

            def value(j, m, bank, par):
                c, t = m // 2, m % 2
                pe.wait_ge(ctx_lo, nth(j, 1, 0))
                pe.wait_ge(ctx_rest, nth(j, 1, 0))
                if isinstance(j, int) and j == 0 and m == 0:
                    pe.wait_ge(w_hi, BY_VECTOR)
                    pe.wait_ge(w_lo_dve, BY_VECTOR)
                hi, lo = cT[par]
                rows = slice(t * P, (t + 1) * P)
                cols = slice(D + c * 512, D + (c + 1) * 512)
                return products(bank[:, :], [
                    (hi[:, 0, rows], wkv0_s[0][:, cols]), (lo[:, rows], wkv0_s[0][:, cols]),
                    (hi[:, 0, rows], wkv0_s[1][:, cols]),
                    (hi[:, 1, rows], wkvr_s[0][:, cols]), (hi[:, 1, rows], wkvr_s[1][:, cols])])

            def turn(src, bank):
                for t in range(2):
                    for a in range(2):
                        mm = pe.transpose(bank[:, a * N2 + t * P:a * N2 + (t + 1) * P],
                                          src[:, t, a * P:(a + 1) * P], ident[:, :])
                return mm

            def gate(j, bank, par):
                pe.wait_ge(drained["turn_x1"], nth(j, 1, 0))
                if isinstance(j, int) and j == 0:
                    pe.wait_ge(gate_w_ready, 2)
                return products(bank[:, 0:N2], [(wgate[:, a, :], part[:, a, :]) for a in range(2) for part in x1T[par]])

            def turn_gate(j, bank):
                pe.wait_ge(drained["gate"], nth(j, 1, 0))
                for t in range(2):
                    mm = pe.transpose(bank[:, t * P:(t + 1) * P], gate_s[:, t * P:(t + 1) * P], ident[:, :])
                return mm

            def expert(j, k, bank, par):
                t, c = k // 4, k % 4
                if isinstance(j, int) and j == 0 and k == 0:
                    pe.wait_ge(w_lo_pool, 3)
                terms = []
                for a in range(2):
                    terms += three(x1T[par], wexp_s, lambda y: y[:, a, t * P:(t + 1) * P],
                                   lambda w: w[:, a, c * 512:(c + 1) * 512])
                return products(bank[:, :], terms)

            def combine(j, bank):
                pe.wait_ge(drained["turn_mixed"], nth(j, 1, 0))
                if isinstance(j, int) and j == 0:
                    pe.wait_ge(w_lo_pool, 4)
                for t in range(2):
                    terms = []
                    for a in range(2):
                        terms += three(mT_s, wcomb_s, lambda m: m[:, a, t * P:(t + 1) * P], lambda w: w[:, a, :])
                    mm = products(bank[:, t * C:(t + 1) * C], terms)
                return mm

            def general(i, u, position, par):
                for n, (slot, pos, kind, k, off) in enumerate(JOBS):
                    j = plus(i, off)
                    if slot != u or pos != position or not exists(j, pairs):
                        continue
                    bank_free(pe, i, n)
                    bank, jp = gen_ps[n % BANKS], (par + off) % 2
                    if kind == "expert":
                        mm = expert(j, k, bank, jp)
                    elif kind == "value":
                        mm = value(j, k, bank, jp)
                    elif kind == "turn_x":
                        pe.wait_ge(xn_done, nth(j, 1, 0))
                        mm = turn(x_raw, bank)
                    elif kind == "turn_x1":
                        pe.wait_ge(xn2_done, nth(j, 1, 0))
                        mm = turn(xn2, bank)
                    elif kind == "turn_mixed":
                        pe.wait_ge(mixed_done, nth(j, 2, 1))
                        mm = turn(mixed, bank)
                    elif kind == "gate":
                        mm = gate(j, bank, jp)
                    elif kind == "turn_gate":
                        mm = turn_gate(j, bank)
                    else:
                        mm = combine(j, bank)
                    mm.then_inc(made[kind], 1)

            pe.wait_ge(const_b, 1)

            def step(i, par):
                now, before, nxt = exists(i, pairs), exists(plus(i, -1), pairs), exists(i + 1, pairs)
                for u in range(SLOTS):
                    if now:
                        scores(i, u)
                    if u == 0 and before:
                        turn_probs(i - 1, 7)
                    if u > 0 and now:
                        turn_probs(i, u - 1)
                    if u < 6 and now:
                        queries_keys(i, u + 2, par)
                    if u >= 6 and nxt:
                        queries_keys(i + 1, u - 6, (par + 1) % 2)
                    general(i, u, "mid", par)
                    if u < 2 and before:
                        project(i - 1, 6 + u)
                    if u >= 2 and now:
                        project(i, u - 2)
                    if u == 0 and before:
                        attend(i - 1, 7)
                    if u > 0 and now:
                        attend(i, u - 1)
                    general(i, u, "late", par)

            steps(pe, pairs, step)

        def previous_expert(i, u):
            for slot, _, kind, k, off in JOBS:
                if kind == "expert" and slot == (u - 1) % SLOTS:
                    off -= u == 0
                    if exists(plus(i, off), pairs):
                        return k, plus(i, off), off
            return None

        @block.scalar
        def _(act):
            def split_hi(sem_in, count, pieces, done):
                act.wait_ge(sem_in, count)
                for to, of in pieces:
                    last = act.copy(to, of)
                last.then_inc(done, 1)

            def keys_values_ctx(j, par):
                act.wait_ge(c_in, (j + 1) * 16)
                wait(act, made["value"], nth(j, 4, 3 - 8))
                wait(act, qk_made, nth(j, HEAD_PAIRS, 7 - 16))
                act.copy(cT[par][0][:, :, :], c_raw[:, :, :]).then_inc(ctx_hi, 1)

            def exps(j, p):
                act.wait_ge(max_done, nth(j, HEAD_PAIRS, p))
                wait(act, pT_made, nth(j, HEAD_PAIRS, p - 2))
                wait(act, inv_done, nth(j, HEAD_PAIRS, p - 2))
                for k in range(4):
                    last = act.activation(probs[p % 2][:, k, :], s_ps[:, k * P:(k + 1) * P], ACT.Exp,
                                          bias=neg_max[p % 2][:, k:k + 1], accum_out=sums[p % 2][:, k:k + 1])
                last.then_inc(exp_done, 1)

            def qk(j, p):
                wait(act, s_made, nth(j, HEAD_PAIRS, p - 2))
                bank, kh = qk_ps, k_s[p % 2][0]
                split_hi(qk_made, nth(j, HEAD_PAIRS, p), [
                    (q_s[p % 2][0][:, :], bank[:, 0:N2]),
                    (kh[0:HALF, :, 0:P], bank[0:HALF, N2:].rearrange("p (t n) -> p t n", t=2)),
                    (kh[HALF:P, :, P:N2], bank[HALF:P, N2:].rearrange("p (t n) -> p t n", t=2))], qk_hi)

            def pT(j, p):
                wait(act, o_made, nth(j, HEAD_PAIRS, p - 1))
                split_hi(pT_made, nth(j, HEAD_PAIRS, p), [(pT_s[0][:, :], pT_ps[:, :])], pT_hi)

            def attended(j, p):
                wait(act, proj_made, nth(j, HEAD_PAIRS, p - 2))
                bank, oh = o_ps[:, :].rearrange("p (t n) -> p t n", t=2), o_s[p % 2][0]
                split_hi(o_made, nth(j, HEAD_PAIRS, p), [
                    (oh[0:HALF, :, :], bank[0:HALF, :, 0:P]), (oh[HALF:P, :, :], bank[HALF:P, :, P:N2])], o_hi)

            def tanh(j, k):
                act.wait_ge(drained["expert"], nth(j, 8, k))
                wait(act, mix_done, nth(j, 8, k - 2))
                act.activation(th[k % 2], z[k % 2], ACT.Tanh, scale=0.5).then_inc(tanh_done, 1)

            def tanh_plus_one(j, k):
                act.wait_ge(tanh_done, nth(j, 8, k))
                act.activation(th[k % 2], th[k % 2], ACT.Copy, bias=1.0).then_inc(tanh_plus, 1)

            def general(i, u, par):
                for kind, k, j, off, b in jobs(u, "mid", i):
                    bank, jp = gen_ps[b], (par + off) % 2
                    if kind == "value":
                        c, t = k // 2, k % 2
                        wait(act, o_made, nth(j, HEAD_PAIRS, 3 + 4 * c - 8))
                        split_hi(made[kind], nth(j, 4, k), [(v_s[0][:, t, c * 512:(c + 1) * 512], bank[:, :])], hi_of[kind])
                    elif kind in ("turn_x", "turn_x1", "turn_mixed"):
                        if kind == "turn_x":
                            to = xT[jp][0]
                            wait(act, qk_made, nth(j, HEAD_PAIRS, 7 - 16))
                        elif kind == "turn_x1":
                            to = x1T[jp][0]
                            wait(act, made["expert"], nth(j, 8, 7 - 16))
                        else:
                            to = mT_s[0]
                            wait(act, made["combine"], plus(j, 0))
                        split_hi(made[kind], nth(j, 1, 0), [(to[:, :, :].rearrange("p a n -> p (a n)"), bank[:, :])],
                                 hi_of[kind])

            def gate_exps(j):
                act.wait_ge(top_done, nth(j, 1, 0))
                for t in range(2):
                    last = act.activation(gate_exp[:, t, :], top8[:, t, :], ACT.Exp,
                                          bias=neg_top[:, t:t + 1], accum_out=gate_sum[:, t:t + 1])
                last.then_inc(gate_exp_done, 1)

            def step(i, par):
                now, before, nxt = exists(i, pairs), exists(plus(i, -1), pairs), exists(i + 1, pairs)
                for u in range(SLOTS):
                    if u == 0 and before:
                        pT(i - 1, 7)
                    if u > 0 and now:
                        pT(i, u - 1)
                    if now:
                        exps(i, u)
                    if u == 6 and before:
                        gate_exps(i - 1)
                    e = previous_expert(i, u)
                    if u == 3 and nxt:
                        keys_values_ctx(i + 1, (par + 1) % 2)
                    if u < 6 and now:
                        qk(i, u + 2)
                    if u >= 6 and nxt:
                        qk(i + 1, u - 6)
                    if e is not None:
                        tanh(e[1], e[0])
                    general(i, u, par)
                    if e is not None:
                        tanh_plus_one(e[1], e[0])
                    if u == 0 and before:
                        attended(i - 1, 7)
                    if u > 0 and now:
                        attended(i, u - 1)
                    if isinstance(i, int) and i == 0 and u < 4:
                        weight_hi(act, 3 + u)

            act.wait_ge(zeroed, 1)
            for n in range(BY_VECTOR):
                weight_hi(act, n)
            act.wait_ge(small_in, 48)
            act.wait_ge(zeroed, 2)
            act.copy(wgate[:, :, 0:E], gate_raw[:, :, :]).then_inc(gate_w_ready, 1)
            steps(act, pairs, step)

        @block.vector
        def _(dve):
            def split_lo(hi_sem, count, pieces, done):
                dve.wait_ge(hi_sem, count)
                for lo, of, hi in pieces:
                    last = dve.tensor_tensor(lo, of, hi.bitcast(F32), ALU.subtract)
                last.then_inc(done, 1)

            def norm_stats(j, n, src):
                for t in range(2):
                    dve.bn_stats(stats[n][:, t, :], src[:, t, :]).then_inc(bn_done[n], 1)

            def stats_ready(j, n):
                dve.wait_ge(bn_done[n], nth(j, 2, 1))
                wait(dve, (xn_done, xn2_done)[n], plus(j, 0))

            def norm_merge(j, n):
                for t in range(2):
                    dve.bn_aggr(mv[n][:, t, :], stats[n][:, t, :]).then_inc(mv_done[n], 1)

            def normalise(j, n, src, to, done):
                dve.wait_ge(rstd_done[n], nth(j, 1, 0))
                for t in range(2):
                    last = dve.tensor_scalar(to[:, t, :], src[:, t, :], mv[n][:, t, 0:1], rstd[n][:, t:t + 1],
                                             ALU.subtract, ALU.mult)
                last.then_inc(done, 1)

            def rest_lo(j, par):
                dve.wait_ge(ctx_hi, nth(j, 1, 0))
                rest = cT[par][0][HALF:P, 1, :]
                dve.tensor_tensor(rest, c_raw[HALF:P, 1, :], rest.bitcast(F32), ALU.subtract).then_inc(ctx_rest, 1)

            def row_max(j, p):
                dve.wait_ge(s_made, nth(j, HEAD_PAIRS, p))
                wait(dve, exp_done, nth(j, HEAD_PAIRS, p - 2))
                dve.tensor_reduce(neg_max[p % 2][:, :], s_ps[:, :].rearrange("p (k n) -> p k n", k=4), AX_X,
                                  ALU.max, negate=True).then_inc(max_done, 1)

            def inverse(j, p):
                dve.wait_ge(exp_done, nth(j, HEAD_PAIRS, p))
                wait(dve, probs_done, nth(j, HEAD_PAIRS, p - 2))
                dve.reciprocal(inv_sums[p % 2][:, :], sums[p % 2][:, :]).then_inc(inv_done, 1)

            def qk(j, p):
                bank, (kh, kl) = qk_ps, k_s[p % 2]
                split_lo(qk_hi, nth(j, HEAD_PAIRS, p), [
                    (q_s[p % 2][1][:, :], bank[:, 0:N2], q_s[p % 2][0][:, :]),
                    (kl[0:HALF, :, 0:P], bank[0:HALF, N2:].rearrange("p (t n) -> p t n", t=2), kh[0:HALF, :, 0:P]),
                    (kl[HALF:P, :, P:N2], bank[HALF:P, N2:].rearrange("p (t n) -> p t n", t=2), kh[HALF:P, :, P:N2])],
                    qk_lo)

            def pT(j, p):
                split_lo(pT_hi, nth(j, HEAD_PAIRS, p), [(pT_s[1][:, :], pT_ps[:, :], pT_s[0][:, :])], pT_lo)

            def attended(j, p):
                bank, (oh, ol) = o_ps[:, :].rearrange("p (t n) -> p t n", t=2), o_s[p % 2]
                split_lo(o_hi, nth(j, HEAD_PAIRS, p), [
                    (ol[0:HALF, :, :], bank[0:HALF, :, 0:P], oh[0:HALF, :, :]),
                    (ol[HALF:P, :, :], bank[HALF:P, :, P:N2], oh[HALF:P, :, :])], o_lo)

            def expert_bias(j, k, par):
                c = k % 4
                dve.wait_ge(made["expert"], nth(j, 8, k))
                if isinstance(j, int) and j == 0 and k == 0:
                    dve.wait_ge(w_hi, 7)
                    dve.wait_ge(w_lo_pool, 4)
                    dve.wait_ge(small_in, 48)
                wait(dve, silu_done, nth(j, 8, k - 2))
                b = expert_bank[k]
                dve.tensor_tensor(z[k % 2], gen_ps[b][:, :], ebias[:, c * 512:(c + 1) * 512],
                                  ALU.add).then_inc(drained["expert"], 1)

            expert_bank = {k: n % BANKS for n, (_, _, kind, k, _) in enumerate(JOBS) if kind == "expert"}

            def add_residual(j, par):
                dve.wait_ge(proj_made, nth(j, HEAD_PAIRS, 7))
                dve.wait_ge(xb_done, nth(j, 1, 0))
                flat_x1, flat_xb = (y[:, :, :].rearrange("p t c -> p (t c)") for y in (x1[par], xb))
                dve.tensor_tensor(flat_x1, proj_ps[:, :], flat_xb, ALU.add).then_inc(x1_done, 1)

            def gate_logits(j, bank):
                dve.wait_ge(made["turn_gate"], nth(j, 1, 0))
                parts = bank[:, 0:N2].rearrange("p (t n) -> p t n", t=2)[:, :, 0:2 * E]
                for t in range(2):
                    last = dve.tensor_reduce(logits[:, t, :], parts[:, t, :].rearrange("p (h e) -> p e h", h=2),
                                             AX_X, ALU.add)
                last.then_inc(drained["turn_gate"], 1)

            def logits_ready(j):
                dve.wait_ge(drained["turn_gate"], nth(j, 1, 0))
                wait(dve, gate_exp_done, plus(j, 0))

            def link(ins, j, n):
                ins.then_inc(route_step, 1)
                dve.wait_ge(route_step, nth(j, 6, n))

            def route_top(j):
                for t in range(2):
                    last = dve.max(top8[:, t, :], logits[:, t, :])
                link(last, j, 0)
                dve.tensor_scalar(neg_top[:, :], top8[:, :, 0], -1.0, None, ALU.mult).then_inc(top_done, 1)
                for t in range(2):
                    last = dve.max_index(top_at[:, t, :], top8[:, t, :], logits[:, t, :])
                link(last, j, 1)
                link(dve.tensor_copy(top_atf[:, :, :], top_at[:, :, 0:2]), j, 2)
                dve.tensor_tensor(chosen[:, :, :], expert_no[:, :].unsqueeze(1).broadcast_to([P, 4, E]),
                                  top_atf[:, :, :].rearrange("p t k -> p (t k)").unsqueeze(2).broadcast_to([P, 4, E]),
                                  ALU.is_equal)

            def route_weights(j, par):
                dve.wait_ge(gate_exp_done, nth(j, 1, 0))
                link(dve.reciprocal(gate_inv[:, :], gate_sum[:, :]), j, 3)
                link(dve.scalar_tensor_tensor(out=top_w[:, :, :], in0=gate_exp[:, :, 0:2], scalar=0.5,
                                              in1=gate_inv[:, :].unsqueeze(2).broadcast_to([P, 2, 2]),
                                              op0=ALU.mult, op1=ALU.mult), j, 4)
                link(dve.tensor_tensor(chosen[:, :, :], chosen[:, :, :],
                                       top_w[:, :, :].rearrange("p t k -> p (t k)").unsqueeze(2).broadcast_to([P, 4, E]),
                                       ALU.mult), j, 5)
                wait(dve, mix_done, nth(j, 8, 7 - 16))
                both = chosen[:, :, :].rearrange("p (t k) e -> p t k e", k=2)
                dve.tensor_tensor(route_w[par][:, :, :], both[:, :, 0, :], both[:, :, 1, :],
                                  ALU.add).then_inc(route_done, 1)

            def general(i, u, par):
                for kind, k, j, off, b in jobs(u, "mid", i):
                    bank, jp = gen_ps[b], (par + off) % 2
                    if kind == "value":
                        c, t = k // 2, k % 2
                        cols = slice(c * 512, (c + 1) * 512)
                        split_lo(hi_of[kind], nth(j, 4, k), [(v_s[1][:, t, cols], bank[:, :], v_s[0][:, t, cols])],
                                 drained[kind])
                    elif kind in ("turn_x", "turn_x1", "turn_mixed"):
                        hi, lo = {"turn_x": xT[jp], "turn_x1": x1T[jp], "turn_mixed": mT_s}[kind]
                        flat2 = "p a n -> p (a n)"
                        split_lo(hi_of[kind], nth(j, 1, 0), [
                            (lo[:, :, :].rearrange(flat2), bank[:, :], hi[:, :, :].rearrange(flat2))], drained[kind])
                    elif kind == "gate":
                        dve.wait_ge(made[kind], nth(j, 1, 0))
                        wait(dve, made["turn_gate"], plus(j, 0))
                        dve.tensor_copy(gate_s[:, :], bank[:, 0:N2]).then_inc(drained[kind], 1)
                    elif kind == "turn_gate":
                        gate_logits(j, bank)
                    elif kind == "combine":
                        dve.wait_ge(made[kind], nth(j, 1, 0))
                        wait(dve, out_stored, j * 16)
                        dve.tensor_tensor(outb[:, :, :].rearrange("p t c -> p (t c)"), bank[:, :],
                                          x1[jp][:, :, :].rearrange("p t c -> p (t c)"),
                                          ALU.add).then_inc(drained[kind], 1)

            def step(i, par):
                now, before, nxt = exists(i, pairs), exists(plus(i, -1), pairs), exists(i + 1, pairs)
                nxtp = (par + 1) % 2
                for u in range(SLOTS):
                    e = previous_expert(i, u)
                    if now:
                        row_max(i, u)
                    if u == 6 and before:
                        logits_ready(i - 1)
                    if u == 3 and before:
                        wait(dve, made["turn_x1"], i - 1)
                        normalise(i - 1, 1, x1[nxtp], xn2, xn2_done)
                    if u < 2 and before:
                        attended(i - 1, 6 + u)
                    if u >= 2 and now:
                        attended(i, u - 2)
                    if u == 2 and before:
                        add_residual(i - 1, nxtp)
                    if u == 6 and before:
                        route_top(i - 1)
                    if u == 0 and before:
                        pT(i - 1, 7)
                    if u > 0 and now:
                        pT(i, u - 1)
                    if e is not None:
                        expert_bias(e[1], e[0], (par + e[2]) % 2)
                    if u == 0 and nxt:
                        dve.wait_ge(x_in, (i + 2) * 16)
                        norm_stats(i + 1, 0, x_raw)
                    if u == 2 and before:
                        dve.wait_ge(x1_done, nth(i - 1, 1, 0))
                        norm_stats(i - 1, 1, x1[nxtp])
                    if u == 0 and nxt:
                        stats_ready(i + 1, 0)
                    if u == 2 and before:
                        stats_ready(i - 1, 1)
                    if u == 4 and nxt:
                        rest_lo(i + 1, nxtp)
                    if now:
                        inverse(i, u)
                    if u == 3 and nxt:
                        normalise(i + 1, 0, x_raw, x_raw, xn_done)
                    if u == 0 and nxt:
                        norm_merge(i + 1, 0)
                    if u == 2 and before:
                        norm_merge(i - 1, 1)
                    if u < 6 and now:
                        qk(i, u + 2)
                    if u >= 6 and nxt:
                        qk(i + 1, u - 6)
                    if u == 6 and before:
                        route_weights(i - 1, nxtp)
                    general(i, u, par)

            for e in range(E):
                last = dve.memset(expert_no[:, e:e + 1], float(e))
            last.then_inc(const_a, 1)
            dve.memset(wkvr_s[1][HALF:P, :].bitcast(F32), 0.0)
            for n in range(BY_VECTOR):
                weight_lo(dve, n, w_lo_dve)
            dve.wait_ge(gate_w_ready, 1)
            dve.tensor_tensor(wgate[:, :, E:2 * E], gate_raw[:, :, :], wgate[:, :, 0:E].bitcast(F32),
                              ALU.subtract).then_inc(gate_w_ready, 1)
            dve.wait_ge(const_a, 1)
            steps(dve, pairs, step)

        @block.gpsimd
        def _(pool):
            def split_ctx_lo(j, par):
                pool.wait_ge(ctx_hi, nth(j, 1, 0))
                hi, lo = cT[par]
                pool.tensor_tensor(lo[:, :], c_raw[:, 0, :], hi[:, 0, :].bitcast(F32),
                                   ALU.subtract).then_inc(ctx_lo, 1)

            def rsqrt(j, n):
                pool.wait_ge(mv_done[n], nth(j, 2, 1))
                wait(pool, rstd_done[n], plus(j, 0))
                pool.tensor_tensor(var_eps[n][:, :], mv[n][:, :, 1], eps[:, :], ALU.add).then_inc(eps_done[n], 1)
                pool.wait_ge(eps_done[n], nth(j, 1, 0))
                pool.tensor_tensor(rstd[n][:, :], var_eps[n][:, :], minus_half[:, :], ALU.pow).then_inc(rstd_done[n], 1)

            def normalise_probs(j, p):
                pool.wait_ge(inv_done, nth(j, HEAD_PAIRS, p))
                b = p % 2
                pool.tensor_tensor(probs[b][:, :, :], probs[b][:, :, :],
                                   inv_sums[b][:, :].unsqueeze(2).broadcast_to([P, 4, P]),
                                   ALU.mult).then_inc(probs_done, 1)

            def silu(j, k):
                pool.wait_ge(tanh_plus, nth(j, 8, k))
                pool.tensor_tensor(th[k % 2], th[k % 2], z[k % 2], ALU.mult).then_inc(silu_done, 1)

            def mix(j, k, par):
                t, c = k // 4, k % 4
                pool.wait_ge(silu_done, nth(j, 8, k))
                pool.wait_ge(route_done, nth(j, 1, 0))
                src = th[k % 2].rearrange("p (e c) -> p e c", e=2)
                w = route_w[par][:, t, 2 * c:2 * c + 2].unsqueeze(2).broadcast_to([P, 2, C])
                if c == 0:
                    wait(pool, mixed_done, nth(j, 2, t - 1))
                    pool.tensor_tensor(acc.rearrange("p (e c) -> p e c", e=2), src, w, ALU.mult).then_inc(mix_done, 1)
                    return
                adds = 6 * 1
                wait(pool, mix_step, nth(j, adds, 3 * t + c - 2))
                pool.tensor_tensor(weighted.rearrange("p (e c) -> p e c", e=2), src, w, ALU.mult).then_inc(mix_done, 1)
                pool.wait_ge(mix_done, nth(j, 8, k))
                pool.tensor_tensor(acc, acc, weighted, ALU.add).then_inc(mix_step, 1)
                if c == 3:
                    pool.wait_ge(mix_step, nth(j, adds, 3 * t + 2))
                    wait(pool, made["turn_mixed"], plus(j, 0))
                    pool.tensor_tensor(mixed[:, t, :], acc[:, 0:C], acc[:, C:2 * C], ALU.add).then_inc(mixed_done, 1)

            def add_proj_bias(j):
                pool.wait_ge(xres_in, (j + 1) * 16)
                for t in range(2):
                    last = pool.tensor_tensor(xb[:, t, :], xb[:, t, :], pbias[:, :], ALU.add)
                last.then_inc(xb_done, 1)

            def step(i, par):
                now, before, nxt = exists(i, pairs), exists(plus(i, -1), pairs), exists(i + 1, pairs)
                nxtp = (par + 1) % 2
                for u in range(SLOTS):
                    if u == 1 and nxt:
                        rsqrt(i + 1, 0)
                    if now:
                        normalise_probs(i, u)
                    if u == 2 and before:
                        rsqrt(i - 1, 1)
                    if (e := previous_expert(i, u)) is not None:
                        silu(e[1], e[0])
                        mix(e[1], e[0], (par + e[2]) % 2)
                    if u == 3 and nxt:
                        split_ctx_lo(i + 1, nxtp)
                    if u == 5 and now:
                        add_proj_bias(i)
                    if isinstance(i, int) and i == 0 and u < 4:
                        weight_lo(pool, 3 + u, w_lo_pool)

            for b in range(2):
                for part in k_s[b]:
                    pool.memset(part[:, :, :].bitcast(F32), 0.0)
            pool.memset(wgate[:, :, :].bitcast(F32), 0.0)
            pool.memset(eps[:, :], EPS)
            pool.memset(minus_half[:, :], -0.5).then_inc(zeroed, 2)
            pool.memset(ident[:, :], 0.0).then_inc(const_b, 1)
            pool.wait_ge(const_b, 1)
            pool.affine_select(out=ident[:, :], in_=ident[:, :], compare_op=ALU.not_equal, fill=1.0, base=0,
                               pattern=[[-1, P]], channel_multiplier=1).then_inc(const_b, 1)
            pool.wait_ge(small_in, 48)
            steps(pool, pairs, step)


def kernel(x, ctx_768, L0_xattn_Wq, L0_xattn_Wkv, L0_xattn_Wproj, L0_xattn_bproj, L0_ffn_gate_w,
           L0_ffn_expert_w, L0_ffn_expert_b, L0_ffn_combine_w):
    import numpy as np
    import concourse.bacc as bacc
    from concourse.bass_utils import run_bass_kernel_spmd

    x, ctx, wkv = np.asarray(x), np.asarray(ctx_768), np.asarray(L0_xattn_Wkv)
    B, S, C = x.shape
    K = ctx.shape[2]
    ctx_pairs = ctx.reshape(B // 2, 2 * S, K).transpose(0, 2, 1)
    rest = ctx_pairs[:, 128:, :]
    ctxT = np.concatenate([ctx_pairs[:, :128, :], np.concatenate([rest, rest], axis=1)], axis=2)
    arrays = {
        "x": x.reshape(B * S, C),
        "ctxT": ctxT,
        "wq": np.asarray(L0_xattn_Wq),
        "wkv": wkv,
        "wkv_rest": np.concatenate([wkv[128:], wkv[128:]], axis=0),
        "wproj": np.asarray(L0_xattn_Wproj),
        "bproj": np.asarray(L0_xattn_bproj),
        "gateT": np.asarray(L0_ffn_gate_w).T,
        "expertT": np.asarray(L0_ffn_expert_w).transpose(2, 0, 1).reshape(C, -1),
        "expert_b": np.asarray(L0_ffn_expert_b).reshape(-1),
        "combineT": np.asarray(L0_ffn_combine_w).T,
    }
    arrays = {f"in_{k}": np.ascontiguousarray(v) for k, v in arrays.items()}
    nc = bacc.Bacc("TRN2", target_bir_lowering=False, num_devices=1)
    args = [nc.dram_tensor(k, v.shape, mybir.dt.from_np(v.dtype), kind="ExternalInput").ap() for k, v in arrays.items()]
    args.append(nc.dram_tensor("out_dram", (B * S, C), F32, kind="ExternalOutput").ap())
    xattn_moe_kernel(nc, *args)
    got = run_bass_kernel_spmd(nc, [arrays], core_ids=[0]).results[0]["out_dram"]
    return got.reshape(B, S, C)
```

```python
from contextlib import ExitStack

import concourse.bass as bass
from concourse import mybir

P = 128
F32 = mybir.dt.float32
F32R = mybir.dt.float32r
U32 = mybir.dt.uint32
ALU = mybir.AluOpType
ACT = mybir.ActivationFunctionType
AX_X = mybir.AxisListType.X

HALF = 64
HEAD_PAIRS = 8
SLOTS = HEAD_PAIRS
EPS = 1e-5

JOBS = [
    (0, "mid", "combine", 0, -3),
    (0, "late", "expert", 3, -2),
    (1, "mid", "value", 2, 0),
    (1, "late", "expert", 4, -2),
    (2, "mid", "value", 3, 0),
    (2, "late", "expert", 5, -2),
    (3, "mid", "turn_x1", 0, -1),
    (3, "late", "expert", 6, -2),
    (4, "mid", "gate", 0, -1),
    (4, "mid", "turn_x", 0, 1),
    (4, "late", "expert", 7, -2),
    (5, "mid", "turn_gate", 0, -1),
    (5, "mid", "value", 0, 1),
    (5, "late", "expert", 0, -1),
    (6, "mid", "value", 1, 1),
    (6, "late", "expert", 1, -1),
    (7, "mid", "turn_mixed", 0, -2),
    (7, "late", "expert", 2, -1),
]
BANKS = 3
PER_PAIR = {"expert": 8, "value": 4, "turn_x": 1, "turn_x1": 1, "gate": 1, "turn_gate": 1,
            "turn_mixed": 1, "combine": 1}


def plus(j, n):
    return j + n if n else j


def nth(j, per, k):
    return plus(j * per if per != 1 else j, k + 1)


def exists(j, pairs):
    return not isinstance(j, int) or 0 <= j < pairs


def wait(eng, sem, count):
    if not isinstance(count, int) or count > 0:
        eng.wait_ge(sem, count)


def steps(eng, pairs, step):
    for i in (-1, 0, 1, 2, 3):
        step(i, i % 2)
    with eng.Fori(4, pairs - 3, 2) as i:
        step(i, 0)
        step(i + 1, 1)
    for i in (pairs - 2, pairs - 1, pairs, pairs + 1, pairs + 2):
        step(i, i % 2)


def xattn_moe_kernel(nc, x, ctxT, wq, wkv, wkv_rest, wproj, bproj, gateT, expertT, expert_b, combineT, out):
    pairs = x.shape[0] // (2 * P)
    C = x.shape[1]
    D = wq.shape[1]
    E = gateT.shape[1]
    N2 = 2 * P

    x_pairs = x.rearrange("(j t p) c -> j p t c", t=2, p=P)
    out_pairs = out.rearrange("(j t p) c -> j p t c", t=2, p=P)

    with ExitStack() as stack:
        def sb(name, shape, dt=F32):
            return stack.enter_context(nc.sbuf_tensor(name, shape, dt))

        def sem(name):
            return stack.enter_context(nc.semaphore(name))

        def hilo(name, shape):
            return [sb(name + "_hi", shape, F32R), sb(name + "_lo", shape, F32R)]

        wq_s = hilo("wq_s", [P, 2, D])
        wkv0_s = hilo("wkv0_s", [P, 2 * D])
        wkvr_s = hilo("wkvr_s", [P, 2 * D])
        wproj_s = hilo("wproj_s", [P, HEAD_PAIRS, C])
        wexp_s = hilo("wexp_s", [P, 2, E * C])
        wcomb_s = hilo("wcomb_s", [P, 2, C])
        wgate = sb("wgate", [P, 2, P], F32R)
        gate_raw = sb("gate_raw", [P, 2, E])
        ebias = sb("ebias", [P, E * C])
        pbias = sb("pbias", [P, C])
        ident = sb("ident", [P, P])
        minus_half = sb("minus_half", [P, 2])
        eps = sb("eps", [P, 2])
        expert_no = sb("expert_no", [P, E])

        x_raw = sb("x_raw", [P, 2, C])
        c_raw = sb("c_raw", [P, 2, N2])
        xT = [hilo(f"xT{b}", [P, 2, N2]) for b in range(2)]
        cT = [(sb(f"cT{b}_hi", [P, 2, N2], F32R), sb(f"cT{b}_lo", [P, N2], F32R)) for b in range(2)]
        v_s = hilo("v_s", [P, 2, D])
        q_s = [hilo(f"q_s{b}", [P, N2]) for b in range(2)]
        k_s = [hilo(f"k_s{b}", [P, 2, N2]) for b in range(2)]
        probs = [sb(f"probs{b}", [P, 4, P]) for b in range(2)]
        pT_s = hilo("pT_s", [P, 4 * P])
        o_s = [hilo(f"o_s{b}", [P, 2, P]) for b in range(2)]
        later = sb("later", [P, 4, 2 * C])
        *x1, xb, outb = [later[:, n, :].rearrange("p (t c) -> p t c", t=2) for n in range(4)]
        x1T = [hilo(f"x1T{b}", [P, 2, N2]) for b in range(2)]
        mT_s = hilo("mT_s", [P, 2, N2])
        gate_s = sb("gate_s", [P, N2])
        scratch = sb("scratch", [P, 2, 2048])
        z = [scratch[:, 0, 0:512], scratch[:, 0, 512:1024]]
        th = [scratch[:, 0, 1024:1536], scratch[:, 0, 1536:2048]]
        acc = scratch[:, 1, 0:512]
        weighted = scratch[:, 1, 512:1024]
        mixed = scratch[:, 1, 1024:1536].rearrange("p (t c) -> p t c", t=2)
        xn2 = scratch[:, 1, 1536:2048].rearrange("p (t c) -> p t c", t=2)

        stats = [sb(f"stats{n}", [P, 2, 6]) for n in (1, 2)]
        mv = [sb(f"mv{n}", [P, 2, 2]) for n in (1, 2)]
        var_eps = [sb(f"var_eps{n}", [P, 2]) for n in (1, 2)]
        rstd = [sb(f"rstd{n}", [P, 2]) for n in (1, 2)]
        neg_max = [sb(f"neg_max{b}", [P, 4]) for b in range(2)]
        sums = [sb(f"sums{b}", [P, 4]) for b in range(2)]
        inv_sums = [sb(f"inv_sums{b}", [P, 4]) for b in range(2)]
        logits = sb("logits", [P, 2, E])
        top8 = sb("top8", [P, 2, 8])
        top_at = sb("top_at", [P, 2, 8], U32)
        top_atf = sb("top_atf", [P, 2, 2])
        neg_top = sb("neg_top", [P, 2])
        gate_exp = sb("gate_exp", [P, 2, 8])
        gate_sum = sb("gate_sum", [P, 2])
        gate_inv = sb("gate_inv", [P, 2])
        top_w = sb("top_w", [P, 2, 2])
        chosen = sb("chosen", [P, 4, E])
        route_w = [sb(f"route_w{b}", [P, 2, E]) for b in range(2)]

        qk_ps = stack.enter_context(nc.psum_tensor("qk_ps", [P, 512], F32))
        s_ps = stack.enter_context(nc.psum_tensor("s_ps", [P, 512], F32))
        pT_ps = stack.enter_context(nc.psum_tensor("pT_ps", [P, 512], F32))
        o_ps = stack.enter_context(nc.psum_tensor("o_ps", [P, 512], F32))
        proj_ps = stack.enter_context(nc.psum_tensor("proj_ps", [P, 512], F32))
        gen_ps = [stack.enter_context(nc.psum_tensor(f"gen_ps{b}", [P, 512], F32)) for b in range(BANKS)]

        x_in, c_in, xres_in, gate_in, bias_in, out_stored = (
            sem(n) for n in ("x_in", "c_in", "xres_in", "gate_in", "bias_in", "out_stored"))
        w_in = [sem(f"w_in{n}") for n in range(7)]
        const_a, const_b, zeroed = sem("const_a"), sem("const_b"), sem("zeroed")
        w_hi, w_lo_dve, w_lo_pool, gate_w_ready = (
            sem(n) for n in ("w_hi", "w_lo_dve", "w_lo_pool", "gate_w_ready"))
        qk_made, s_made, pT_made, o_made, proj_made = (
            sem(n) for n in ("qk_made", "s_made", "pT_made", "o_made", "proj_made"))
        made = {k: sem("made_" + k) for k in PER_PAIR}
        qk_hi, exp_done, pT_hi, o_hi, ctx_hi, tanh_done, tanh_plus, gate_exp_done = (
            sem(n) for n in ("qk_hi", "exp_done", "pT_hi", "o_hi", "ctx_hi", "tanh_done", "tanh_plus", "gate_exp_done"))
        hi_of = {k: sem("hi_" + k) for k in ("value", "turn_x", "turn_x1", "turn_mixed")}
        qk_lo, max_done, inv_done, pT_lo, o_lo, x1_done, xn_done, xn2_done, ctx_rest = (
            sem(n) for n in ("qk_lo", "max_done", "inv_done", "pT_lo", "o_lo", "x1_done", "xn_done",
                             "xn2_done", "ctx_rest"))
        drained = {k: sem("drained_" + k) for k in PER_PAIR}
        bn_done = [sem(f"bn_done{n}") for n in (1, 2)]
        mv_done = [sem(f"mv_done{n}") for n in (1, 2)]
        top_done, route_step, route_done = sem("top_done"), sem("route_step"), sem("route_done")
        tail_silu_done, tail_mix_first, tail_mix_done = (
            sem(n) for n in ("tail_silu_done", "tail_mix_first", "tail_mix_done"))
        ctx_lo, probs_done, xb_done, silu_done, mix_step, mix_done, mixed_done = (
            sem(n) for n in ("ctx_lo", "probs_done", "xb_done", "silu_done", "mix_step", "mix_done", "mixed_done"))
        eps_done = [sem(f"eps_done{n}") for n in (1, 2)]
        rstd_done = [sem(f"rstd_done{n}") for n in (1, 2)]

        block = stack.enter_context(nc.Block())

        def jobs(u, position, i):
            for n, (slot, pos, kind, k, off) in enumerate(JOBS):
                if slot == u and pos == position and exists(plus(i, off), pairs):
                    yield kind, k, plus(i, off), off, n % BANKS

        def bank_free(pe, i, n):
            m = n
            while True:
                m -= BANKS
                step_back = -(m // len(JOBS))
                _, _, kind, k, off = JOBS[m % len(JOBS)]
                j = plus(i, off - step_back)
                if exists(j, pairs):
                    pe.wait_ge(drained[kind], nth(j, PER_PAIR[kind], k))
                    return
                if isinstance(i, int) and i - step_back < -1:
                    return

        def tail_no(j, k):
            if isinstance(j, int) and j >= pairs - 2 and (j - (pairs - 2)) * 8 + k >= 4:
                return (j - (pairs - 2)) * 8 + k - 4
            return None

        def job_done(eng, by_pool, in_tail, j, k):
            while k < 0:
                j, k = plus(j, -1), k + 8
            if (n := tail_no(j, k)) is not None:
                eng.wait_ge(in_tail, n + 1)
            elif exists(j, pairs):
                eng.wait_ge(by_pool, nth(j, 8, k))

        raw = [scratch[:, 0, :], scratch[:, 1, :], ebias[:, :], later[:, :, :].rearrange("p n c -> p (n c)"),
               scratch[:, 0, :], scratch[:, 1, :], later[:, 3, :]]
        WEIGHTS = [
            (wq.rearrange("(a p) n -> p a n", p=P), raw[0].rearrange("p (a n) -> p a n", a=2)),
            (wkv[0:P, :], raw[1]),
            (wkv_rest, raw[2]),
            (wproj.rearrange("(g p) n -> p g n", p=P), raw[3].rearrange("p (g n) -> p g n", g=HEAD_PAIRS)),
            (expertT[0:P, :], raw[4]),
            (expertT[P:2 * P, :], raw[5]),
            (combineT.rearrange("(a p) n -> p a n", p=P), raw[6].rearrange("p (a n) -> p a n", a=2)),
        ]
        whole = slice(0, 2 * D)
        SPLIT = [
            (0, whole, *[w[:, :, :].rearrange("p a n -> p (a n)") for w in wq_s]),
            (1, whole, *[w[:, :] for w in wkv0_s]),
            (2, whole, *[w[:, :] for w in wkvr_s]),
            (3, whole, *[w[:, :, :].rearrange("p g n -> p (g n)") for w in wproj_s]),
        ]
        for a in range(2):
            for q in range(4):
                cols = slice(q * 512, (q + 1) * 512)
                SPLIT.append((4 + a, cols, *[w[:, a, cols] for w in wexp_s]))
        SPLIT.append((6, slice(0, 2 * C), *[w[:, :, :].rearrange("p a n -> p (a n)") for w in wcomb_s]))
        BY_VECTOR, EXPERTS_SPLIT = 3, len(SPLIT) - 1
        QSCALE = float(HALF) ** -0.5

        def weight_hi(act, n):
            which, cols, hi, _ = SPLIT[n]
            act.wait_ge(w_in[which], 16)
            act.activation(hi, raw[which][:, cols], ACT.Copy, scale=QSCALE if n == 0 else 1.0).then_inc(w_hi, 1)

        def weight_lo(eng, n, done):
            eng.wait_ge(w_hi, n + 1)
            which, cols, hi, lo = SPLIT[n]
            if n == 0:
                eng.scalar_tensor_tensor(out=lo, in0=raw[0], scalar=QSCALE, in1=hi.bitcast(F32),
                                         op0=ALU.mult, op1=ALU.subtract).then_inc(done, 1)
            else:
                rows = HALF if n == 2 else P
                eng.tensor_tensor(lo[0:rows, :], raw[which][0:rows, cols], hi[0:rows, :].bitcast(F32),
                                  ALU.subtract).then_inc(done, 1)

        @block.sync
        def _(sp):
            def load_x(j):
                wait(sp, made["turn_x"], j)
                sp.dma_start(x_raw[:, :, :], x_pairs[j]).then_inc(x_in, 16)

            def load_ctx(j):
                wait(sp, ctx_hi, j)
                wait(sp, ctx_lo, j)
                wait(sp, ctx_rest, j)
                sp.dma_start(c_raw[:, :, :], ctxT[j].rearrange("p (a n) -> p a n", a=2)).then_inc(c_in, 16)

            def load_weights(n):
                if n in (4, 5):
                    sp.wait_ge(w_lo_dve, n - 3)
                elif n == 6:
                    sp.wait_ge(w_lo_pool, 1)
                of, to = WEIGHTS[n]
                sp.dma_start(to, of).then_inc(w_in[n], 16)

            load_x(0)
            load_ctx(0)
            for n in range(4):
                load_weights(n)
            sp.dma_start(gate_raw[:, :, :], gateT.rearrange("(a p) e -> p a e", p=P)).then_inc(gate_in, 16)
            sp.dma_start(pbias[:, :], bproj.partition_broadcast(P)).then_inc(bias_in, 16)
            load_weights(4)
            load_weights(5)
            sp.wait_ge(w_lo_dve, BY_VECTOR)
            sp.dma_start(ebias[:, :], expert_b.partition_broadcast(P)).then_inc(bias_in, 16)

            def step(i, par):
                if exists(plus(i, -3), pairs):
                    sp.wait_ge(drained["combine"], i - 2)
                    sp.dma_start(out_pairs[i - 3], outb[:, :, :]).then_inc(out_stored, 16)
                if exists(i, pairs):
                    if isinstance(i, int) and i == 0:
                        sp.wait_ge(w_lo_pool, 1)
                    wait(sp, x1_done, i)
                    sp.dma_start(xb[:, :, :], x_pairs[i]).then_inc(xres_in, 16)
                if exists(i + 2, pairs):
                    load_ctx(i + 2)
                    load_x(i + 2)
                if isinstance(i, int) and i == 0:
                    load_weights(6)

            steps(sp, pairs, step)
            sp.wait_ge(out_stored, 16 * pairs)

        @block.tensor
        def _(pe):
            def products(out_ap, terms, start=True, stop=True, skip=False):
                for n, (l, r) in enumerate(terms):
                    mm = pe.matmul(out_ap, l, r, start=start and n == 0, stop=stop and n == len(terms) - 1,
                                   skip_group_check=skip)
                return mm

            def three(lhs, rhs, pick_l, pick_r):
                return [(pick_l(lhs[a]), pick_r(rhs[b])) for a, b in ((0, 0), (0, 1), (1, 0))]

            def queries_keys(j, p, par):
                if p == 0:
                    pe.wait_ge(drained["turn_x"], nth(j, 1, 0))
                if isinstance(j, int) and j == 0 and p == 0:
                    pe.wait_ge(w_hi, BY_VECTOR)
                    pe.wait_ge(w_lo_dve, BY_VECTOR)
                wait(pe, qk_lo, nth(j, HEAD_PAIRS, p - 1))
                cols = slice(p * P, (p + 1) * P)
                bank = qk_ps
                terms = []
                for a in range(2):
                    terms += three(wq_s, xT[par], lambda w: w[:, a, cols], lambda y: y[:, a, :])
                products(bank[:, 0:N2], terms)
                hi, lo = cT[par]
                products(bank[:, N2:2 * N2], [
                    (wkv0_s[0][:, cols], hi[:, 0, :]), (wkv0_s[0][:, cols], lo[:, :]), (wkv0_s[1][:, cols], hi[:, 0, :]),
                    (wkvr_s[0][:, cols], hi[:, 1, :]), (wkvr_s[1][:, cols], hi[:, 1, :]),
                ]).then_inc(qk_made, 1)

            def scores(j, p):
                pe.wait_ge(qk_lo, nth(j, HEAD_PAIRS, p))
                wait(pe, exp_done, nth(j, HEAD_PAIRS, p - 1))
                for t in range(2):
                    mm = products(s_ps[:, t * N2:(t + 1) * N2], three(
                        q_s[p % 2], k_s[p % 2], lambda q: q[:, t * P:(t + 1) * P], lambda k: k[:, t, :]))
                mm.then_inc(s_made, 1)

            def turn_probs(j, p):
                pe.wait_ge(probs_done, nth(j, HEAD_PAIRS, p))
                wait(pe, pT_lo, nth(j, HEAD_PAIRS, p - 1))
                for k in range(4):
                    mm = pe.transpose(pT_ps[:, k * P:(k + 1) * P], probs[p % 2][:, k, :], ident[:, :])
                mm.then_inc(pT_made, 1)

            def attend(j, p):
                pe.wait_ge(pT_lo, nth(j, HEAD_PAIRS, p))
                if p % 4 == 0:
                    pe.wait_ge(drained["value"], nth(j, 4, 2 * (p // 4) + 1))
                wait(pe, o_lo, nth(j, HEAD_PAIRS, p - 1))
                for t in range(2):
                    mm = products(o_ps[:, t * N2:(t + 1) * N2], three(
                        v_s, pT_s, lambda v: v[:, t, p * P:(p + 1) * P], lambda q: q[:, t * N2:(t + 1) * N2]))
                mm.then_inc(o_made, 1)

            def project(j, p):
                pe.wait_ge(o_lo, nth(j, HEAD_PAIRS, p))
                if p == 0:
                    wait(pe, x1_done, j)
                    if isinstance(j, int) and j == 0:
                        pe.wait_ge(w_lo_pool, 1)
                for t in range(2):
                    mm = products(proj_ps[:, t * C:(t + 1) * C], three(
                        o_s[p % 2], wproj_s, lambda o: o[:, t, :], lambda w: w[:, p, :]),
                        start=p == 0 and t == 0, stop=p == HEAD_PAIRS - 1, skip=True)
                mm.then_inc(proj_made, 1)

            def value(j, m, bank, par):
                c, t = m // 2, m % 2
                pe.wait_ge(ctx_lo, nth(j, 1, 0))
                pe.wait_ge(ctx_rest, nth(j, 1, 0))
                if isinstance(j, int) and j == 0 and m == 0:
                    pe.wait_ge(w_hi, BY_VECTOR)
                    pe.wait_ge(w_lo_dve, BY_VECTOR)
                hi, lo = cT[par]
                rows = slice(t * P, (t + 1) * P)
                cols = slice(D + c * 512, D + (c + 1) * 512)
                return products(bank[:, :], [
                    (hi[:, 0, rows], wkv0_s[0][:, cols]), (lo[:, rows], wkv0_s[0][:, cols]),
                    (hi[:, 0, rows], wkv0_s[1][:, cols]),
                    (hi[:, 1, rows], wkvr_s[0][:, cols]), (hi[:, 1, rows], wkvr_s[1][:, cols])])

            def turn(src, bank):
                for t in range(2):
                    for a in range(2):
                        mm = pe.transpose(bank[:, a * N2 + t * P:a * N2 + (t + 1) * P],
                                          src[:, t, a * P:(a + 1) * P], ident[:, :])
                return mm

            def gate(j, bank, par):
                pe.wait_ge(drained["turn_x1"], nth(j, 1, 0))
                if isinstance(j, int) and j == 0:
                    pe.wait_ge(gate_w_ready, 2)
                return products(bank[:, 0:N2], [(wgate[:, a, :], part[:, a, :]) for a in range(2) for part in x1T[par]])

            def turn_gate(j, bank):
                pe.wait_ge(drained["gate"], nth(j, 1, 0))
                for t in range(2):
                    mm = pe.transpose(bank[:, t * P:(t + 1) * P], gate_s[:, t * P:(t + 1) * P], ident[:, :])
                return mm

            def expert(j, k, bank, par):
                t, c = k // 4, k % 4
                if isinstance(j, int) and j == 0 and k == 0:
                    pe.wait_ge(w_lo_pool, EXPERTS_SPLIT - BY_VECTOR)
                terms = []
                for a in range(2):
                    terms += three(x1T[par], wexp_s, lambda y: y[:, a, t * P:(t + 1) * P],
                                   lambda w: w[:, a, c * 512:(c + 1) * 512])
                return products(bank[:, :], terms)

            def combine(j, bank):
                pe.wait_ge(drained["turn_mixed"], nth(j, 1, 0))
                if isinstance(j, int) and j == 0:
                    pe.wait_ge(w_lo_pool, len(SPLIT) - BY_VECTOR)
                for t in range(2):
                    terms = []
                    for a in range(2):
                        terms += three(mT_s, wcomb_s, lambda m: m[:, a, t * P:(t + 1) * P], lambda w: w[:, a, :])
                    mm = products(bank[:, t * C:(t + 1) * C], terms)
                return mm

            def general(i, u, position, par):
                for n, (slot, pos, kind, k, off) in enumerate(JOBS):
                    j = plus(i, off)
                    if slot != u or pos != position or not exists(j, pairs):
                        continue
                    bank_free(pe, i, n)
                    bank, jp = gen_ps[n % BANKS], (par + off) % 2
                    if kind == "expert":
                        mm = expert(j, k, bank, jp)
                    elif kind == "value":
                        mm = value(j, k, bank, jp)
                    elif kind == "turn_x":
                        pe.wait_ge(xn_done, nth(j, 1, 0))
                        mm = turn(x_raw, bank)
                    elif kind == "turn_x1":
                        pe.wait_ge(xn2_done, nth(j, 1, 0))
                        mm = turn(xn2, bank)
                    elif kind == "turn_mixed":
                        if (n := tail_no(j, 7)) is not None:
                            pe.wait_ge(mixed_done, nth(pairs - 2, 2, 0))
                            pe.wait_ge(tail_mix_done, n + 1)
                        else:
                            pe.wait_ge(mixed_done, nth(j, 2, 1))
                        mm = turn(mixed, bank)
                    elif kind == "gate":
                        mm = gate(j, bank, jp)
                    elif kind == "turn_gate":
                        mm = turn_gate(j, bank)
                    else:
                        mm = combine(j, bank)
                    mm.then_inc(made[kind], 1)

            pe.wait_ge(const_b, 1)

            def step(i, par):
                now, before, nxt = exists(i, pairs), exists(plus(i, -1), pairs), exists(i + 1, pairs)
                for u in range(SLOTS):
                    if now:
                        scores(i, u)
                    if u == 0 and before:
                        turn_probs(i - 1, 7)
                    if u > 0 and now:
                        turn_probs(i, u - 1)
                    if u < 6 and now:
                        queries_keys(i, u + 2, par)
                    if u >= 6 and nxt:
                        queries_keys(i + 1, u - 6, (par + 1) % 2)
                    general(i, u, "mid", par)
                    if u < 2 and before:
                        project(i - 1, 6 + u)
                    if u >= 2 and now:
                        project(i, u - 2)
                    if u == 0 and before:
                        attend(i - 1, 7)
                    if u > 0 and now:
                        attend(i, u - 1)
                    general(i, u, "late", par)

            steps(pe, pairs, step)

        def previous_expert(i, u, back=1):
            for slot, _, kind, k, off in JOBS:
                if kind == "expert" and slot == (u - back) % SLOTS:
                    off -= u < back
                    if exists(plus(i, off), pairs):
                        return k, plus(i, off), off
            return None

        @block.scalar
        def _(act):
            def split_hi(sem_in, count, pieces, done):
                act.wait_ge(sem_in, count)
                for to, of in pieces:
                    last = act.copy(to, of)
                last.then_inc(done, 1)

            def split_ctx_hi(j, par):
                act.wait_ge(c_in, (j + 1) * 16)
                wait(act, made["value"], nth(j, 4, 3 - 8))
                wait(act, qk_made, nth(j, HEAD_PAIRS, 7 - 16))
                act.copy(cT[par][0][:, :, :], c_raw[:, :, :]).then_inc(ctx_hi, 1)

            def exps(j, p):
                act.wait_ge(max_done, nth(j, HEAD_PAIRS, p))
                wait(act, pT_made, nth(j, HEAD_PAIRS, p - 2))
                wait(act, inv_done, nth(j, HEAD_PAIRS, p - 2))
                for k in range(4):
                    last = act.activation(probs[p % 2][:, k, :], s_ps[:, k * P:(k + 1) * P], ACT.Exp,
                                          bias=neg_max[p % 2][:, k:k + 1], accum_out=sums[p % 2][:, k:k + 1])
                last.then_inc(exp_done, 1)

            def qk(j, p):
                wait(act, s_made, nth(j, HEAD_PAIRS, p - 2))
                bank, kh = qk_ps, k_s[p % 2][0]
                split_hi(qk_made, nth(j, HEAD_PAIRS, p), [
                    (q_s[p % 2][0][:, :], bank[:, 0:N2]),
                    (kh[0:HALF, :, 0:P], bank[0:HALF, N2:].rearrange("p (t n) -> p t n", t=2)),
                    (kh[HALF:P, :, P:N2], bank[HALF:P, N2:].rearrange("p (t n) -> p t n", t=2))], qk_hi)

            def pT(j, p):
                wait(act, o_made, nth(j, HEAD_PAIRS, p - 1))
                split_hi(pT_made, nth(j, HEAD_PAIRS, p), [(pT_s[0][:, :], pT_ps[:, :])], pT_hi)

            def attended(j, p):
                wait(act, proj_made, nth(j, HEAD_PAIRS, p - 2))
                bank, oh = o_ps[:, :].rearrange("p (t n) -> p t n", t=2), o_s[p % 2][0]
                split_hi(o_made, nth(j, HEAD_PAIRS, p), [
                    (oh[0:HALF, :, :], bank[0:HALF, :, 0:P]), (oh[HALF:P, :, :], bank[HALF:P, :, P:N2])], o_hi)

            def tanh(j, k):
                act.wait_ge(drained["expert"], nth(j, 8, k))
                job_done(act, mix_done, tail_mix_done, j, k - 2)
                act.activation(th[k % 2], z[k % 2], ACT.Tanh, scale=0.5).then_inc(tanh_done, 1)

            def tanh_plus_one(j, k):
                act.wait_ge(tanh_done, nth(j, 8, k))
                act.activation(th[k % 2], th[k % 2], ACT.Copy, bias=1.0).then_inc(tanh_plus, 1)

            def general(i, u, par):
                for kind, k, j, off, b in jobs(u, "mid", i):
                    bank, jp = gen_ps[b], (par + off) % 2
                    if kind == "value":
                        c, t = k // 2, k % 2
                        wait(act, o_made, nth(j, HEAD_PAIRS, 3 + 4 * c - 8))
                        split_hi(made[kind], nth(j, 4, k), [(v_s[0][:, t, c * 512:(c + 1) * 512], bank[:, :])], hi_of[kind])
                    elif kind in ("turn_x", "turn_x1", "turn_mixed"):
                        if kind == "turn_x":
                            to = xT[jp][0]
                            wait(act, qk_made, nth(j, HEAD_PAIRS, 7 - 16))
                        elif kind == "turn_x1":
                            to = x1T[jp][0]
                            wait(act, made["expert"], nth(j, 8, 7 - 16))
                        else:
                            to = mT_s[0]
                            wait(act, made["combine"], plus(j, 0))
                        split_hi(made[kind], nth(j, 1, 0), [(to[:, :, :].rearrange("p a n -> p (a n)"), bank[:, :])],
                                 hi_of[kind])

            def gate_exps(j):
                act.wait_ge(top_done, nth(j, 1, 0))
                for t in range(2):
                    last = act.activation(gate_exp[:, t, :], top8[:, t, :], ACT.Exp,
                                          bias=neg_top[:, t:t + 1], accum_out=gate_sum[:, t:t + 1])
                last.then_inc(gate_exp_done, 1)

            def step(i, par):
                now, before, nxt = exists(i, pairs), exists(plus(i, -1), pairs), exists(i + 1, pairs)
                for u in range(SLOTS):
                    if u == 0 and before:
                        pT(i - 1, 7)
                    if u > 0 and now:
                        pT(i, u - 1)
                    if now:
                        exps(i, u)
                    if u == 6 and before:
                        gate_exps(i - 1)
                    e = previous_expert(i, u)
                    if u == 3 and nxt:
                        split_ctx_hi(i + 1, (par + 1) % 2)
                    if u < 6 and now:
                        qk(i, u + 2)
                    if u >= 6 and nxt:
                        qk(i + 1, u - 6)
                    if e is not None:
                        tanh(e[1], e[0])
                    general(i, u, par)
                    if e is not None and tail_no(e[1], e[0]) is None:
                        tanh_plus_one(e[1], e[0])
                    if u == 0 and before:
                        attended(i - 1, 7)
                    if u > 0 and now:
                        attended(i, u - 1)
                    if isinstance(i, int) and i == -1 and u == 4:
                        for n in range(BY_VECTOR + 1):
                            weight_hi(act, n)
                        act.wait_ge(gate_in, 16)
                        act.copy(wgate[:, :, 0:E], gate_raw[:, :, :]).then_inc(gate_w_ready, 1)
                    if isinstance(i, int) and i == 0:
                        weight_hi(act, 4 + u)
                    if isinstance(i, int) and i == 1 and u == 0:
                        weight_hi(act, EXPERTS_SPLIT)

            act.wait_ge(zeroed, 2)
            act.activation(neg_top[:, :], minus_half[:, :], ACT.Exp)
            steps(act, pairs, step)

        @block.vector
        def _(dve):
            def split_lo(hi_sem, count, pieces, done):
                dve.wait_ge(hi_sem, count)
                for lo, of, hi in pieces:
                    last = dve.tensor_tensor(lo, of, hi.bitcast(F32), ALU.subtract)
                last.then_inc(done, 1)

            def norm_stats(j, n, src):
                for t in range(2):
                    dve.bn_stats(stats[n][:, t, :], src[:, t, :]).then_inc(bn_done[n], 1)

            def stats_ready(j, n):
                dve.wait_ge(bn_done[n], nth(j, 2, 1))
                wait(dve, (xn_done, xn2_done)[n], plus(j, 0))

            def norm_merge(j, n):
                for t in range(2):
                    dve.bn_aggr(mv[n][:, t, :], stats[n][:, t, :]).then_inc(mv_done[n], 1)

            def normalise(j, n, src, to, done):
                dve.wait_ge(rstd_done[n], nth(j, 1, 0))
                for t in range(2):
                    last = dve.tensor_scalar(to[:, t, :], src[:, t, :], mv[n][:, t, 0:1], rstd[n][:, t:t + 1],
                                             ALU.subtract, ALU.mult)
                last.then_inc(done, 1)

            def rest_lo(j, par):
                dve.wait_ge(ctx_hi, nth(j, 1, 0))
                rest = cT[par][0][HALF:P, 1, :]
                dve.tensor_tensor(rest, c_raw[HALF:P, 1, :], rest.bitcast(F32), ALU.subtract).then_inc(ctx_rest, 1)

            def row_max(j, p):
                dve.wait_ge(s_made, nth(j, HEAD_PAIRS, p))
                wait(dve, exp_done, nth(j, HEAD_PAIRS, p - 2))
                dve.tensor_reduce(neg_max[p % 2][:, :], s_ps[:, :].rearrange("p (k n) -> p k n", k=4), AX_X,
                                  ALU.max, negate=True).then_inc(max_done, 1)

            def inverse(j, p):
                dve.wait_ge(exp_done, nth(j, HEAD_PAIRS, p))
                wait(dve, probs_done, nth(j, HEAD_PAIRS, p - 2))
                dve.reciprocal(inv_sums[p % 2][:, :], sums[p % 2][:, :]).then_inc(inv_done, 1)

            def qk(j, p):
                bank, (kh, kl) = qk_ps, k_s[p % 2]
                split_lo(qk_hi, nth(j, HEAD_PAIRS, p), [
                    (q_s[p % 2][1][:, :], bank[:, 0:N2], q_s[p % 2][0][:, :]),
                    (kl[0:HALF, :, 0:P], bank[0:HALF, N2:].rearrange("p (t n) -> p t n", t=2), kh[0:HALF, :, 0:P]),
                    (kl[HALF:P, :, P:N2], bank[HALF:P, N2:].rearrange("p (t n) -> p t n", t=2), kh[HALF:P, :, P:N2])],
                    qk_lo)

            def pT(j, p):
                split_lo(pT_hi, nth(j, HEAD_PAIRS, p), [(pT_s[1][:, :], pT_ps[:, :], pT_s[0][:, :])], pT_lo)

            def attended(j, p):
                bank, (oh, ol) = o_ps[:, :].rearrange("p (t n) -> p t n", t=2), o_s[p % 2]
                split_lo(o_hi, nth(j, HEAD_PAIRS, p), [
                    (ol[0:HALF, :, :], bank[0:HALF, :, 0:P], oh[0:HALF, :, :]),
                    (ol[HALF:P, :, :], bank[HALF:P, :, P:N2], oh[HALF:P, :, :])], o_lo)

            def expert_bias(j, k, par):
                c = k % 4
                dve.wait_ge(made["expert"], nth(j, 8, k))
                if isinstance(j, int) and j == 0 and k == 0:
                    dve.wait_ge(w_hi, EXPERTS_SPLIT)
                    dve.wait_ge(w_lo_pool, EXPERTS_SPLIT - BY_VECTOR)
                    dve.wait_ge(bias_in, 32)
                job_done(dve, silu_done, tail_silu_done, j, k - 2)
                b = expert_bank[k]
                dve.tensor_tensor(z[k % 2], gen_ps[b][:, :], ebias[:, c * 512:(c + 1) * 512],
                                  ALU.add).then_inc(drained["expert"], 1)

            def silu_and_mix(j, k, par):
                t, c, n = k // 4, k % 4, tail_no(j, k)
                dve.wait_ge(tanh_done, nth(j, 8, k))
                dve.scalar_tensor_tensor(out=th[k % 2], in0=th[k % 2], scalar=1.0, in1=z[k % 2], op0=ALU.add,
                                         op1=ALU.mult).then_inc(tail_silu_done, 1)
                dve.wait_ge(tail_silu_done, n + 1)
                if c == 0:
                    dve.wait_ge(route_done, nth(j, 1, 0))
                    dve.wait_ge(made["turn_mixed"], j)
                for h in range(2):
                    src, w = th[k % 2][:, h * C:(h + 1) * C], route_w[par][:, t, 2 * c + h:2 * c + h + 1]
                    if c == 0 and h == 0:
                        last = dve.tensor_scalar(mixed[:, t, :], src, w, None, ALU.mult)
                    else:
                        if h == 0:
                            dve.wait_ge(tail_mix_done, n)
                        else:
                            dve.wait_ge(tail_mix_first, n + 1)
                        last = dve.scalar_tensor_tensor(out=mixed[:, t, :], in0=src, scalar=w, in1=mixed[:, t, :],
                                                        op0=ALU.mult, op1=ALU.add)
                    last.then_inc(tail_mix_done if h else tail_mix_first, 1)

            expert_bank = {k: n % BANKS for n, (_, _, kind, k, _) in enumerate(JOBS) if kind == "expert"}

            def add_residual(j, par):
                dve.wait_ge(proj_made, nth(j, HEAD_PAIRS, 7))
                dve.wait_ge(xb_done, nth(j, 1, 0))
                flat_x1, flat_xb = (y[:, :, :].rearrange("p t c -> p (t c)") for y in (x1[par], xb))
                dve.tensor_tensor(flat_x1, proj_ps[:, :], flat_xb, ALU.add).then_inc(x1_done, 1)

            def gate_logits(j, bank):
                dve.wait_ge(made["turn_gate"], nth(j, 1, 0))
                parts = bank[:, 0:N2].rearrange("p (t n) -> p t n", t=2)[:, :, 0:2 * E]
                for t in range(2):
                    last = dve.tensor_reduce(logits[:, t, :], parts[:, t, :].rearrange("p (h e) -> p e h", h=2),
                                             AX_X, ALU.add)
                last.then_inc(drained["turn_gate"], 1)

            def logits_ready(j):
                dve.wait_ge(drained["turn_gate"], nth(j, 1, 0))
                wait(dve, gate_exp_done, plus(j, 0))

            def link(ins, j, n):
                ins.then_inc(route_step, 1)
                dve.wait_ge(route_step, nth(j, 6, n))

            def route_top(j):
                for t in range(2):
                    last = dve.max(top8[:, t, :], logits[:, t, :])
                link(last, j, 0)
                dve.tensor_scalar(neg_top[:, :], top8[:, :, 0], -1.0, None, ALU.mult).then_inc(top_done, 1)
                for t in range(2):
                    last = dve.max_index(top_at[:, t, :], top8[:, t, :], logits[:, t, :])
                link(last, j, 1)
                link(dve.tensor_copy(top_atf[:, :, :], top_at[:, :, 0:2]), j, 2)
                dve.tensor_tensor(chosen[:, :, :], expert_no[:, :].unsqueeze(1).broadcast_to([P, 4, E]),
                                  top_atf[:, :, :].rearrange("p t k -> p (t k)").unsqueeze(2).broadcast_to([P, 4, E]),
                                  ALU.is_equal)

            def route_weights(j, par):
                dve.wait_ge(gate_exp_done, nth(j, 1, 0))
                link(dve.reciprocal(gate_inv[:, :], gate_sum[:, :]), j, 3)
                link(dve.scalar_tensor_tensor(out=top_w[:, :, :], in0=gate_exp[:, :, 0:2], scalar=0.5,
                                              in1=gate_inv[:, :].unsqueeze(2).broadcast_to([P, 2, 2]),
                                              op0=ALU.mult, op1=ALU.mult), j, 4)
                link(dve.tensor_tensor(chosen[:, :, :], chosen[:, :, :],
                                       top_w[:, :, :].rearrange("p t k -> p (t k)").unsqueeze(2).broadcast_to([P, 4, E]),
                                       ALU.mult), j, 5)
                wait(dve, mix_done, nth(j, 8, 7 - 16))
                both = chosen[:, :, :].rearrange("p (t k) e -> p t k e", k=2)
                dve.tensor_tensor(route_w[par][:, :, :], both[:, :, 0, :], both[:, :, 1, :],
                                  ALU.add).then_inc(route_done, 1)

            def general(i, u, par):
                for kind, k, j, off, b in jobs(u, "mid", i):
                    bank, jp = gen_ps[b], (par + off) % 2
                    if kind == "value":
                        c, t = k // 2, k % 2
                        cols = slice(c * 512, (c + 1) * 512)
                        split_lo(hi_of[kind], nth(j, 4, k), [(v_s[1][:, t, cols], bank[:, :], v_s[0][:, t, cols])],
                                 drained[kind])
                    elif kind in ("turn_x", "turn_x1", "turn_mixed"):
                        hi, lo = {"turn_x": xT[jp], "turn_x1": x1T[jp], "turn_mixed": mT_s}[kind]
                        flat2 = "p a n -> p (a n)"
                        split_lo(hi_of[kind], nth(j, 1, 0), [
                            (lo[:, :, :].rearrange(flat2), bank[:, :], hi[:, :, :].rearrange(flat2))], drained[kind])
                    elif kind == "gate":
                        dve.wait_ge(made[kind], nth(j, 1, 0))
                        wait(dve, made["turn_gate"], plus(j, 0))
                        dve.tensor_copy(gate_s[:, :], bank[:, 0:N2]).then_inc(drained[kind], 1)
                    elif kind == "turn_gate":
                        gate_logits(j, bank)
                    elif kind == "combine":
                        dve.wait_ge(made[kind], nth(j, 1, 0))
                        wait(dve, out_stored, j * 16)
                        dve.tensor_tensor(outb[:, :, :].rearrange("p t c -> p (t c)"), bank[:, :],
                                          x1[jp][:, :, :].rearrange("p t c -> p (t c)"),
                                          ALU.add).then_inc(drained[kind], 1)

            def step(i, par):
                now, before, nxt = exists(i, pairs), exists(plus(i, -1), pairs), exists(i + 1, pairs)
                nxtp = (par + 1) % 2
                for u in range(SLOTS):
                    e = previous_expert(i, u)
                    if now:
                        row_max(i, u)
                    if u == 6 and before:
                        logits_ready(i - 1)
                    if u == 3 and before:
                        wait(dve, made["turn_x1"], i - 1)
                        normalise(i - 1, 1, x1[nxtp], xn2, xn2_done)
                    if u < 2 and before:
                        attended(i - 1, 6 + u)
                    if u >= 2 and now:
                        attended(i, u - 2)
                    if u == 2 and before:
                        add_residual(i - 1, nxtp)
                    if u == 6 and before:
                        route_top(i - 1)
                    if u == 0 and before:
                        pT(i - 1, 7)
                    if u > 0 and now:
                        pT(i, u - 1)
                    if e is not None:
                        expert_bias(e[1], e[0], (par + e[2]) % 2)
                    late = previous_expert(i, u, 2)
                    if late is not None and tail_no(late[1], late[0]) is not None:
                        silu_and_mix(late[1], late[0], (par + late[2]) % 2)
                    if u == 0 and nxt:
                        dve.wait_ge(x_in, (i + 2) * 16)
                        norm_stats(i + 1, 0, x_raw)
                    if u == 2 and before:
                        dve.wait_ge(x1_done, nth(i - 1, 1, 0))
                        norm_stats(i - 1, 1, x1[nxtp])
                    if u == 0 and nxt:
                        stats_ready(i + 1, 0)
                    if u == 2 and before:
                        stats_ready(i - 1, 1)
                    if u == 4 and nxt:
                        rest_lo(i + 1, nxtp)
                    if now:
                        inverse(i, u)
                    if u == 3 and nxt:
                        normalise(i + 1, 0, x_raw, x_raw, xn_done)
                    if u == 0 and nxt:
                        norm_merge(i + 1, 0)
                    if u == 2 and before:
                        norm_merge(i - 1, 1)
                    if u < 6 and now:
                        qk(i, u + 2)
                    if u >= 6 and nxt:
                        qk(i + 1, u - 6)
                    if u == 6 and before:
                        route_weights(i - 1, nxtp)
                    general(i, u, par)
                    if isinstance(i, int) and i == -1 and u == 4:
                        for n in range(BY_VECTOR):
                            weight_lo(dve, n, w_lo_dve)
                    if isinstance(i, int) and i == 0 and u == 2:
                        dve.wait_ge(gate_w_ready, 1)
                        dve.tensor_tensor(wgate[:, :, E:2 * E], gate_raw[:, :, :], wgate[:, :, 0:E].bitcast(F32),
                                          ALU.subtract).then_inc(gate_w_ready, 1)

            for e in range(E):
                last = dve.memset(expert_no[:, e:e + 1], float(e))
            last.then_inc(const_a, 1)
            dve.memset(wkvr_s[1][HALF:P, :].bitcast(F32), 0.0)
            dve.wait_ge(const_a, 1)
            steps(dve, pairs, step)

        @block.gpsimd
        def _(pool):
            def split_ctx_lo(j, par):
                pool.wait_ge(ctx_hi, nth(j, 1, 0))
                hi, lo = cT[par]
                pool.tensor_tensor(lo[:, :], c_raw[:, 0, :], hi[:, 0, :].bitcast(F32),
                                   ALU.subtract).then_inc(ctx_lo, 1)

            def rsqrt(j, n):
                pool.wait_ge(mv_done[n], nth(j, 2, 1))
                wait(pool, rstd_done[n], plus(j, 0))
                pool.tensor_tensor(var_eps[n][:, :], mv[n][:, :, 1], eps[:, :], ALU.add).then_inc(eps_done[n], 1)
                pool.wait_ge(eps_done[n], nth(j, 1, 0))
                pool.tensor_tensor(rstd[n][:, :], var_eps[n][:, :], minus_half[:, :], ALU.pow).then_inc(rstd_done[n], 1)

            def normalise_probs(j, p):
                pool.wait_ge(inv_done, nth(j, HEAD_PAIRS, p))
                b = p % 2
                pool.tensor_tensor(probs[b][:, :, :], probs[b][:, :, :],
                                   inv_sums[b][:, :].unsqueeze(2).broadcast_to([P, 4, P]),
                                   ALU.mult).then_inc(probs_done, 1)

            def silu(j, k):
                pool.wait_ge(tanh_plus, nth(j, 8, k))
                pool.tensor_tensor(th[k % 2], th[k % 2], z[k % 2], ALU.mult).then_inc(silu_done, 1)

            def mix(j, k, par):
                t, c = k // 4, k % 4
                pool.wait_ge(silu_done, nth(j, 8, k))
                pool.wait_ge(route_done, nth(j, 1, 0))
                src = th[k % 2].rearrange("p (e c) -> p e c", e=2)
                w = route_w[par][:, t, 2 * c:2 * c + 2].unsqueeze(2).broadcast_to([P, 2, C])
                if c == 0:
                    wait(pool, mixed_done, nth(j, 2, t - 1))
                    pool.tensor_tensor(acc.rearrange("p (e c) -> p e c", e=2), src, w, ALU.mult).then_inc(mix_done, 1)
                    return
                wait(pool, mix_step, nth(j, 6, 3 * t + c - 2))
                pool.tensor_tensor(weighted.rearrange("p (e c) -> p e c", e=2), src, w, ALU.mult).then_inc(mix_done, 1)
                pool.wait_ge(mix_done, nth(j, 8, k))
                pool.tensor_tensor(acc, acc, weighted, ALU.add).then_inc(mix_step, 1)
                if c == 3:
                    pool.wait_ge(mix_step, nth(j, 6, 3 * t + 2))
                    wait(pool, made["turn_mixed"], plus(j, 0))
                    pool.tensor_tensor(mixed[:, t, :], acc[:, 0:C], acc[:, C:2 * C], ALU.add).then_inc(mixed_done, 1)

            def add_proj_bias(j):
                if isinstance(j, int) and j == 0:
                    pool.wait_ge(bias_in, 32)
                pool.wait_ge(xres_in, (j + 1) * 16)
                for t in range(2):
                    last = pool.tensor_tensor(xb[:, t, :], xb[:, t, :], pbias[:, :], ALU.add)
                last.then_inc(xb_done, 1)

            def step(i, par):
                now, before, nxt = exists(i, pairs), exists(plus(i, -1), pairs), exists(i + 1, pairs)
                nxtp = (par + 1) % 2
                for u in range(SLOTS):
                    if u == 1 and nxt:
                        rsqrt(i + 1, 0)
                    if u == 1 and before and not now:
                        rsqrt(i - 1, 1)
                    if now:
                        normalise_probs(i, u)
                    if u == 2 and before and now:
                        rsqrt(i - 1, 1)
                    if (e := previous_expert(i, u)) is not None and tail_no(e[1], e[0]) is None:
                        silu(e[1], e[0])
                        mix(e[1], e[0], (par + e[2]) % 2)
                    if u == 3 and nxt:
                        split_ctx_lo(i + 1, nxtp)
                    if u == 5 and now:
                        add_proj_bias(i)
                    if isinstance(i, int) and i == -1 and u == 4:
                        weight_lo(pool, 3, w_lo_pool)
                    if isinstance(i, int) and i == 0:
                        weight_lo(pool, 4 + u, w_lo_pool)
                    if isinstance(i, int) and i == 1 and u == 0:
                        weight_lo(pool, EXPERTS_SPLIT, w_lo_pool)

            for b in range(2):
                for part in k_s[b]:
                    pool.memset(part[:, :, :].bitcast(F32), 0.0)
            pool.memset(wgate[:, :, :].bitcast(F32), 0.0)
            pool.memset(eps[:, :], EPS)
            pool.memset(minus_half[:, :], -0.5).then_inc(zeroed, 2)
            pool.memset(ident[:, :], 0.0).then_inc(const_b, 1)
            pool.wait_ge(const_b, 1)
            pool.affine_select(out=ident[:, :], in_=ident[:, :], compare_op=ALU.not_equal, fill=1.0, base=0,
                               pattern=[[-1, P]], channel_multiplier=1).then_inc(const_b, 1)
            steps(pool, pairs, step)


def kernel(x, ctx_768, L0_xattn_Wq, L0_xattn_Wkv, L0_xattn_Wproj, L0_xattn_bproj, L0_ffn_gate_w,
           L0_ffn_expert_w, L0_ffn_expert_b, L0_ffn_combine_w):
    import numpy as np
    import concourse.bacc as bacc
    from concourse.bass_utils import run_bass_kernel_spmd

    x, ctx, wkv = np.asarray(x), np.asarray(ctx_768), np.asarray(L0_xattn_Wkv)
    B, S, C = x.shape
    K = ctx.shape[2]
    ctx_pairs = ctx.reshape(B // 2, 2 * S, K).transpose(0, 2, 1)
    rest = ctx_pairs[:, 128:, :]
    ctxT = np.concatenate([ctx_pairs[:, :128, :], np.concatenate([rest, rest], axis=1)], axis=2)
    arrays = {
        "x": x.reshape(B * S, C),
        "ctxT": ctxT,
        "wq": np.asarray(L0_xattn_Wq),
        "wkv": wkv,
        "wkv_rest": np.concatenate([wkv[128:], wkv[128:]], axis=0),
        "wproj": np.asarray(L0_xattn_Wproj),
        "bproj": np.asarray(L0_xattn_bproj),
        "gateT": np.asarray(L0_ffn_gate_w).T,
        "expertT": np.asarray(L0_ffn_expert_w).transpose(2, 0, 1).reshape(C, -1),
        "expert_b": np.asarray(L0_ffn_expert_b).reshape(-1),
        "combineT": np.asarray(L0_ffn_combine_w).T,
    }
    arrays = {f"in_{k}": np.ascontiguousarray(v) for k, v in arrays.items()}
    nc = bacc.Bacc("TRN2", target_bir_lowering=False, num_devices=1)
    args = [nc.dram_tensor(k, v.shape, mybir.dt.from_np(v.dtype), kind="ExternalInput").ap() for k, v in arrays.items()]
    args.append(nc.dram_tensor("out_dram", (B * S, C), F32, kind="ExternalOutput").ap())
    xattn_moe_kernel(nc, *args)
    got = run_bass_kernel_spmd(nc, [arrays], core_ids=[0]).results[0]["out_dram"]
    return got.reshape(B, S, C)
```
